# Optimizing a Trainium2 kernel written in Bass

```python
import numpy as np
import jax
import jax.numpy as jnp

def _softmax(x, axis=-1):
    return jax.nn.softmax(x, axis=axis)

def _gelu(x):
    return jax.nn.gelu(x, approximate=True)

def _silu(x):
    return jax.nn.silu(x)

def _sigmoid(x):
    return jax.nn.sigmoid(x)

def _layernorm(x, axis=-1, eps=1e-05):
    m = jnp.mean(x, axis=axis, keepdims=True)
    v = jnp.var(x, axis=axis, keepdims=True)
    return (x - m) / jnp.sqrt(v + eps)

def _scatter_add(tgt, idx, src, axis=0):
    return tgt.at[idx].add(src)

def _segment_sum(src, seg, n):
    return jax.ops.segment_sum(src, seg, n)
kernel_name = 'mk_gnn_resnorm_d2_gnn_r32_39ccb6'

def setup_inputs(seed: int=0):
    np.random.seed(seed)
    _w = jnp.asarray

    def _rec_inputs():
        import jax
        import jax.numpy as jnp
        _gk = jax.random.key(seed)
        x = -0.000202 + 1 * jax.random.normal(jax.random.fold_in(_gk, 1), (50000, 128), jnp.float32)
        src = jax.random.randint(jax.random.fold_in(_gk, 2), (25000,), 0, 50000, jnp.int32)
        dst = jnp.minimum((50000 * jax.random.uniform(jax.random.fold_in(_gk, 3), (25000,)) ** 2.0).astype(jnp.int32), 49999)
        _o = jnp.argsort(dst, stable=True)
        src = src[_o]
        dst = dst[_o]
        edge_attr_64 = -9.77346e-05 + 0.999888 * jax.random.normal(jax.random.fold_in(_gk, 11), (25000, 64), jnp.float32)
        return (x, src, dst, edge_attr_64)
    x, src, dst, edge_attr_64 = _rec_inputs()

    def _L0_gnn_setup():
        import jax, jax.numpy as jnp
        import numpy as np
        N = 50000
        NE = 25000
        D = 128
        ED = 64
        H = 8
        HD = D // H
        key = jax.random.key(seed)
        ks = jax.random.split(key, 12)
        g = lambda k, shp: jax.random.normal(k, shp, jnp.float32) * 0.05
        return {'V': jax.random.normal(ks[0], (N, D), jnp.float32), 'E': jax.random.normal(ks[1], (NE, ED), jnp.float32), 'edge_index': jax.random.randint(ks[2], (2, NE), 0, N, jnp.int32), 'Wq': g(ks[3], (D, D)), 'bq': jnp.zeros((D,), jnp.float32), 'Wk': g(ks[4], (D, D)), 'bk': jnp.zeros((D,), jnp.float32), 'Wv': g(ks[5], (D, D)), 'bv': jnp.zeros((D,), jnp.float32), 'Wb': g(ks[6], (ED, 1)), 'bb': jnp.zeros((1,), jnp.float32), 'Wo': g(ks[7], (D, D)), 'bo': jnp.zeros((D,), jnp.float32)}
    _L0_gnn_all = _L0_gnn_setup()
    _L0_gnn_in = {k: v for k, v in _L0_gnn_all.items() if k in ('Wq', 'bq', 'Wk', 'bk', 'Wv', 'bv', 'Wb', 'bb', 'Wo', 'bo')}
    del _L0_gnn_all

    def _L1_gnn_setup():
        import jax, jax.numpy as jnp
        import numpy as np
        N_NODES = 50000
        N_EDGES = 25000
        D_IN = 128
        D_OUT = 128
        ALPHA = 0.2
        key = jax.random.key(seed)
        k1, k2, k3, k4 = jax.random.split(key, 4)
        x = jax.random.normal(k1, (N_NODES, D_IN), dtype=jnp.float32)
        W = jax.random.normal(k2, (D_IN, D_OUT), dtype=jnp.float32) * (1.414 / np.sqrt(D_IN))
        a = jax.random.normal(k3, (2 * D_OUT, 1), dtype=jnp.float32) * 0.1
        edge_index = jax.random.randint(k4, (2, N_EDGES), 0, N_NODES, dtype=jnp.int64)
        return {'x': x, 'W': W, 'a': a, 'edge_index': edge_index}
    _L1_gnn_all = _L1_gnn_setup()
    _L1_gnn_in = {k: v for k, v in _L1_gnn_all.items() if k in ('W', 'a')}
    del _L1_gnn_all
    return {'x': x, 'src': src, 'dst': dst, 'edge_attr_64': edge_attr_64, 'L0_gnn_Wq': _L0_gnn_in['Wq'], 'L0_gnn_bq': _L0_gnn_in['bq'], 'L0_gnn_Wk': _L0_gnn_in['Wk'], 'L0_gnn_bk': _L0_gnn_in['bk'], 'L0_gnn_Wv': _L0_gnn_in['Wv'], 'L0_gnn_bv': _L0_gnn_in['bv'], 'L0_gnn_Wb': _L0_gnn_in['Wb'], 'L0_gnn_bb': _L0_gnn_in['bb'], 'L0_gnn_Wo': _L0_gnn_in['Wo'], 'L0_gnn_bo': _L0_gnn_in['bo'], 'L1_gnn_W': _L1_gnn_in['W'], 'L1_gnn_a': _L1_gnn_in['a']}

def reference(x, src, dst, edge_attr_64, L0_gnn_Wq, L0_gnn_bq, L0_gnn_Wk, L0_gnn_bk, L0_gnn_Wv, L0_gnn_bv, L0_gnn_Wb, L0_gnn_bb, L0_gnn_Wo, L0_gnn_bo, L1_gnn_W, L1_gnn_a):
    import jax
    import jax.numpy as jnp

    def _L0_gnn_ref(V, E, edge_index, Wq, bq, Wk, bk, Wv, bv, Wb, bb, Wo, bo):
        import jax, jax.numpy as jnp
        import numpy as np
        N = 50000
        NE = 25000
        D = 128
        ED = 64
        H = 8
        HD = D // H
        src, dest = (edge_index[0], edge_index[1])
        Q = (V[src] @ Wq + bq).reshape(-1, H, HD)
        K = (V[dest] @ Wk + bk).reshape(-1, H, HD)
        Vv = (V[dest] @ Wv + bv).reshape(-1, H, HD)
        bias = E @ Wb + bb
        scores = jnp.einsum('ehd,ehd->eh', Q, K) / np.float32(np.sqrt(HD)) + bias
        m = jax.ops.segment_max(scores, dest, num_segments=N)
        ex = jnp.exp(scores - m[dest])
        den = jax.ops.segment_sum(ex, dest, num_segments=N)
        alpha = ex / den[dest]
        Hagg = jax.ops.segment_sum(alpha[..., None] * Vv, dest, num_segments=N)
        O = Hagg.reshape(N, H * HD) @ Wo + bo
        return O

    def _L1_gnn_ref(x, W, a, edge_index):
        import jax, jax.numpy as jnp
        import numpy as np
        N_NODES = 50000
        N_EDGES = 25000
        D_IN = 128
        D_OUT = 128
        ALPHA = 0.2
        h = x @ W
        src, dst = (edge_index[0], edge_index[1])
        a1 = a[:D_OUT, 0]
        a2 = a[D_OUT:, 0]
        s1 = h @ a1
        s2 = h @ a2
        e = jax.nn.leaky_relu(s1[src] + s2[dst], negative_slope=ALPHA)
        attention = jax.nn.softmax(e)
        msgs = attention[:, None] * h[src]
        output = jax.ops.segment_sum(msgs, dst, num_segments=N_NODES)
        return output
    edge_index = jnp.stack([src, dst])
    x = _layernorm(x + _L0_gnn_ref(x, edge_attr_64, edge_index, L0_gnn_Wq, L0_gnn_bq, L0_gnn_Wk, L0_gnn_bk, L0_gnn_Wv, L0_gnn_bv, L0_gnn_Wb, L0_gnn_bb, L0_gnn_Wo, L0_gnn_bo), axis=-1)
    x = _layernorm(x + _L1_gnn_ref(x, L1_gnn_W, L1_gnn_a, edge_index), axis=-1)
    return x

_drawn_inputs = setup_inputs


def setup_inputs(seed=0):
    import zlib

    import numpy as np

    out = dict(_drawn_inputs(seed))
    spreads = {'L0_gnn_bq': (0.0, 2.0),
     'L0_gnn_bk': (0.0, 2.0),
     'L0_gnn_bv': (0.0, 0.1),
     'L0_gnn_bo': (0.0, 0.1)}
    factors = {'edge_attr_64': 200.0,
     'L0_gnn_Wq': 200.0,
     'L0_gnn_Wk': 200.0,
     'L0_gnn_Wb': 200.0,
     'L1_gnn_W': 200.0,
     'L1_gnn_a': 200.0}
    for name, (base, spread) in spreads.items():
        noise = np.random.default_rng([zlib.crc32(name.encode()), seed]).standard_normal(out[name].shape)
        drawn = base * np.exp(spread * noise) if base else spread * noise
        out[name] = jnp.asarray(drawn.astype(out[name].dtype))
    for name, factor in factors.items():
        out[name] = (out[name] * factor).astype(out[name].dtype)
    return out
```

```python
import concourse.bass as bass
from concourse import mybir
from contextlib import ExitStack


class Step:

    def __init__(self, off, i=None):
        self.off, self.i = off, i
        self.u = off % 2
        uses = (off + 2 - self.u) // 2
        self.g = off if i is None else i * 2 + off
        self.uses = uses if i is None else i + uses

    def back(self, k):
        return Step(self.off - k, self.i)

    def runs(self, groups):
        return self.i is not None or 0 <= self.off < groups


def gnn_kernel(nc, x, src, dst, edge_attr, Wq, bq, Wk, bk, Wv, bv, Wb, bb, Wo, bo, W1, a1, out):
    fp32 = mybir.dt.float32
    i32 = mybir.dt.int32
    ALU = mybir.AluOpType
    ACT = mybir.ActivationFunctionType
    AX = mybir.AxisListType.X

    P = 128
    N, D = x.shape
    NE = src.shape[0]
    ED = edge_attr.shape[1]
    H = 8
    HD = D // H
    G = 4
    TILES = -(-NE // (P * G)) * G
    GROUPS = TILES // G
    EP = P * TILES
    LASTROW = NE - (P - 1) * TILES
    ROWS = (N // P // (GROUPS - 1))
    MAIN = P * ROWS * (GROUPS - 1)
    REST = (N - MAIN) // ROWS
    assert GROUPS % 2 == 1 and REST * ROWS == N - MAIN and REST <= P and 0 < LASTROW <= TILES
    PEEL = 5
    LOOPS = (GROUPS - PEEL) // 2
    GW = G * D
    BW = ROWS * D
    EPS = 1e-5
    BIG = 1e30
    SKIP = 1e5
    SLOPE = 0.2
    CH = H * TILES

    xd_rows = nc.dram_tensor("xd_rows", (EP, D), fp32).ap()
    x1d_rows = nc.dram_tensor("x1d_rows", (EP, D), fp32).ap()
    xs_rows = nc.dram_tensor("xs_rows", (EP, D), fp32).ap()
    x1_table = nc.dram_tensor("x1_table", (N, D), fp32).ap()
    dst_pad = nc.dram_tensor("dst_pad", (EP + 2,), i32)

    def edge_view(a):
        return a.rearrange("(p t) d -> p (t d)", p=P)

    def node_chunk(a, s):
        if s.i is None and s.off == 0:
            return a[MAIN:N, :].rearrange("(p r) d -> p (r d)", r=ROWS)
        return a[0:MAIN, :].rearrange("(p k) d -> p (k d)", p=P)[:, bass.ds((s.g - 1) * BW, BW)]

    def chunk_parts(s):
        return REST if s.i is None and s.off == 0 else P

    with ExitStack() as ctx:
        def sb(name, shape, dt=fp32):
            return ctx.enter_context(nc.sbuf_tensor(name, shape, dt))

        def sem(name):
            return ctx.enter_context(nc.semaphore(name))

        def sem2(name):
            return [sem(f"{name}{u}") for u in range(2)]

        bank = [ctx.enter_context(nc.psum_tensor(f"bank{i}", [P, 512], fp32)) for i in range(8)]

        ident = sb("ident", [P, P])
        ones = sb("ones", [P, P])
        head_sel = sb("head_sel", [P, H])
        expand = sb("expand", [G * H, G, D])
        wq, wk, wv, wo, w1, w1T = (sb(n, [P, D]) for n in ("wq", "wk", "wv", "wo", "w1", "w1T"))
        bcol = sb("bcol", [P, 3])
        bb_col = sb("bb_col", [P, 1])
        wb_row = sb("wb_row", [P, ED])
        bo_row = sb("bo_row", [P, D])
        bo_group = sb("bo_group", [1, GW])
        a_col = sb("a_col", [P, 2])
        a_wide = sb("a_wide", [P, 2, P])
        v_src = sb("v_src", [P, D])
        v_dst = sb("v_dst", [P, D])

        sentinel = sb("sentinel", [1, 96], i32)
        src_tab = sb("src_tab", [P, TILES + 2 * G], i32)
        dst_raw = sb("dst_raw", [P, TILES + 2], i32)
        dst_f = sb("dst_f", [P, TILES + 2])
        dst_tab = sb("dst_tab", [P, TILES + 2 * G], i32)
        dst_cl = sb("dst_cl", [P, TILES])
        same_prev = sb("same_prev", [P, TILES])
        same_next = sb("same_next", [P, TILES])
        first = sb("first", [P, TILES])
        first_last = sb("first_last", [P, TILES])
        at_last_f = sb("at_last_f", [P, TILES])
        at_last2_f = sb("at_last2_f", [P, TILES])
        at_last = sb("at_last", [P, TILES + 2 * G], i32)
        at_last2 = sb("at_last2", [P, TILES + 2 * G], i32)
        carry_idx_f = sb("carry_idx_f", [P, 4])
        carry_idx = sb("carry_idx", [P, 2], i32)
        pen_local = sb("pen_local", [P, H, TILES])
        pen_first = sb("pen_first", [P, TILES])
        pen_pad = sb("pen_pad", [P, TILES])

        edge_in = sb("edge_in", [P, TILES * ED])
        edge_mul = sb("edge_mul", [P, G * ED])
        edge_bias = sb("edge_bias", [P, 2, G])
        idx_slot = sb("idx_slot", [P, 2, 2 * G], i32)
        xs = sb("xs", [P, 2, GW])
        xd = sb("xd", [P, 2, GW])
        xsT = sb("xsT", [P, GW])
        xdT = sb("xdT", [P, 2, GW])
        qT = sb("qT", [P, GW])
        prodT = sb("prodT", [P, GW])
        node_in = sb("node_in", [P, 2, BW])
        node_x1 = sb("node_x1", [P, 2, BW])
        node_out = sb("node_out", [P, 2, BW])
        nst = sb("nst", [P, ROWS, 6])
        nmv = sb("nmv", [P, 2, ROWS, 2])
        nstd = sb("nstd", [P, 2, 2, ROWS])
        nsc = sb("nsc", [P, 2, 2, 2, ROWS])
        eps_cols = sb("eps_cols", [P, 2])

        score = sb("score", [P, H, TILES])
        run_max = sb("run_max", [P, H, TILES])
        tmp = sb("tmp", [P, H, TILES])
        weight = sb("weight", [P, H, TILES])
        decay = sb("decay", [P, H, TILES])
        run_sum = sb("run_sum", [P, H, TILES])
        share = sb("share", [P, TILES, H])
        ends = sb("ends", [P, 2, H])
        factor_row = sb("factor_row", [H, P])
        carry_row = sb("carry_row", [H, 2, P + 1])
        carry_in = sb("carry_in", [P, H])

        share_slot = sb("share_slot", [P, 2, G * H])
        shareT = sb("shareT", [G * H, 2, P])
        vT = sb("vT", [P, 2, GW])
        hT = sb("hT", [P, 2, GW])
        y = sb("y", [P, 2, GW])
        res = sb("res", [P, 2, GW])
        dots = sb("dots", [P, GW])
        yst = sb("yst", [P, G, 6])
        ymv = sb("ymv", [P, 2, G, 2])
        ystd = sb("ystd", [P, 2, G])
        ysc = sb("ysc", [P, 2, 2, G])

        s_src = sb("s_src", [P, TILES])
        s_dst = sb("s_dst", [P, TILES])
        logit = sb("logit", [P, TILES])
        logit2 = sb("logit2", [P, TILES])
        att = sb("att", [P, TILES])
        max_p = sb("max_p", [P, 1])
        max_all = sb("max_all", [1, 1])
        neg_max = sb("neg_max", [P, 1])
        exp_sum = sb("exp_sum", [P, 1])
        inv_sum = sb("inv_sum", [P, 1])
        xa = sb("xa", [P, 2, GW])
        agg = sb("agg", [P, 2, GW])
        aggT = sb("aggT", [P, 2, GW])
        part = sb("part", [P, D])
        diag = sb("diag", [P, P])
        chunkrow = sb("chunkrow", [P, P])
        carryT = sb("carryT", [P, P + 1])
        total = sb("total", [P, D])
        totalT = sb("totalT", [P, D])
        x1c = sb("x1c", [P, D])

        consts_in = sem("consts_in")
        pad_in = sem("pad_in")
        edges_in = sem("edges_in")
        src_in = sem("src_in")
        attr_in = sem("attr_in")
        zeroed = sem("zeroed")
        built = sem("built")
        prep, prep_chain, last_chain = sem("prep"), sem("prep_chain"), sem("last_chain")
        w1T_done, w1T_sb = sem("w1T_done"), sem("w1T_sb")
        v_done = sem("v_done")
        held_pool, held_dve = sem("held_pool"), sem("held_dve")
        idx_ready = sem("idx_ready")
        got_src, got_dst = sem2("got_src"), sem2("got_dst")
        xT_done, xT_sb = sem("xT_done"), sem("xT_sb")
        qk_done, q_sb = sem("qk_done"), sem("q_sb")
        prod_done, s_done, score_done = sem("prod_done"), sem("s_done"), sem("score_done")
        xd_stored = sem2("xd_stored")
        bias_chain, node_chain = sem("bias_chain"), sem("node_chain")
        node_loaded = sem2("node_loaded")
        node_var, node_std, node_ready, node_applied = (
            sem("node_var"), sem("node_std"), sem("node_ready"), sem("node_applied"))
        x1_stored, out_stored = sem2("x1_stored"), sem2("out_stored")
        soft_chain, ends_ready, ends_T = sem("soft_chain"), sem("ends_ready"), sem("ends_T")
        row_ready, carry_T = sem("row_ready"), sem("carry_T")
        args_ready, exps_done = sem("args_ready"), sem("exps_done")
        share_done = sem("share_done")
        xd_back = sem2("xd_back")
        share_cp = sem("share_cp")
        vx_T, vx_Tsb, shT, shT_sb = sem("vx_T"), sem("vx_Tsb"), sem("shT"), sem("shT_sb")
        v_mm, v_sb, x_mm, h_done, o_mm = sem("v_mm"), sem("v_sb"), sem("x_mm"), sem("h_done"), sem("o_mm")
        c_var, c_std, c_fin_chain, node_fin_chain = sem("c_var"), sem("c_std"), sem("c_fin_chain"), sem("node_fin_chain")
        e_var, e_std, e_fin_chain = sem("e_var"), sem("e_std"), sem("e_fin_chain")
        c_chain, c_stats, c_applied, sd_chain, sd_done = (
            sem("c_chain"), sem("c_stats"), sem("c_applied"), sem("sd_chain"), sem("sd_done"))
        c_y = sem("c_y")
        c_scat, x1d_stored = sem2("c_scat"), sem2("x1d_stored")
        d_idx, d_got, d_chain, d_done, xs_stored = sem("d_idx"), sem2("d_got"), sem("d_chain"), sem("d_done"), sem2("xs_stored")
        att_chain, max_col, max_T, max_one, max_b = (
            sem("att_chain"), sem("max_col"), sem("max_T"), sem("max_one"), sem("max_b"))
        neg_ready, exp_done, sum_b, att_ready = sem("neg_ready"), sem("exp_done"), sem("sum_b"), sem("att_ready")
        xs_back, x1d_back = sem2("xs_back"), sem2("x1d_back")
        xa_done, r_chain, r_done = sem("xa_done"), sem("r_chain"), sem("r_done")
        e_T, e_Tsb, e_mm, e_chain, e_stats, e_applied = (
            sem("e_T"), sem("e_Tsb"), sem("e_mm"), sem("e_chain"), sem("e_stats"), sem("e_applied"))
        e_y = sem("e_y")
        e_scat = sem2("e_scat")
        f_dve, f_pe, f_act, f_got, f_scat = sem("f_dve"), sem("f_pe"), sem("f_act"), sem("f_got"), sem("f_scat")

        block = ctx.enter_context(nc.Block())

        def wait(eng, s, value):
            if not isinstance(value, int) or value > 0:
                eng.wait_ge(s, value)

        def hold(eng, s, value):
            wait(eng, s, value)
            if not isinstance(value, int):
                eng.sem_inc(held_pool if eng is nc.gpsimd else held_dve, 1)

        def pipeline(eng, body, tail=0):
            for g in range(PEEL):
                body(Step(g))
            with eng.Fori(0, LOOPS, 1) as i:
                body(Step(PEEL, i))
                body(Step(PEEL + 1, i))
            for g in range(GROUPS, GROUPS + tail):
                body(Step(g))

        class Chain:

            def __init__(self, eng, s, per_step, step=None):
                self.eng, self.sem, self.per, self.k = eng, s, per_step, 0
                self.base = 0 if step is None else step.g * per_step

            def link(self, ins):
                self.k += 1
                assert self.per is None or self.k <= self.per
                ins.then_inc(self.sem, 1)
                hold(self.eng, self.sem, self.base + self.k)

        T = lambda a, u, t: a[:, u, t * D:(t + 1) * D]
        SLOTS_TOTAL = [16 * ((GROUPS + 1) // 2), 16 * (GROUPS // 2)]

        @block.sync
        def _(sp):
            sp.wait_ge(zeroed, 1)
            sp.dma_start(dst_pad[0:1].rearrange("(a b) -> a b", a=1), sentinel[0:1, 0:1]).then_inc(pad_in, 16)
            sp.dma_start(dst_pad[NE + 1:EP + 2].rearrange("(a b) -> a b", a=1),
                         sentinel[0:1, 1:EP + 2 - NE]).then_inc(pad_in, 16)
            sp.dma_start(dst_pad[1:NE + 1].rearrange("(a b) -> a b", a=8),
                         dst.rearrange("(a b) -> a b", a=8)).then_inc(pad_in, 16)
            sp.wait_ge(zeroed, 2)
            head = 112
            main = src[0:head * TILES].rearrange("(p t) -> p t", p=head)
            sp.dma_start(src_tab[0:head, 0:TILES], main).then_inc(src_in, 16)
            sp.dma_start(src_tab[head:P - 1, 0:TILES],
                         src[head * TILES:(P - 1) * TILES].rearrange("(p t) -> p t", t=TILES)).then_inc(src_in, 16)
            sp.dma_start(src_tab[P - 1:P, 0:LASTROW],
                         src[(P - 1) * TILES:NE].rearrange("(p t) -> p t", p=1)).then_inc(src_in, 16)
            sp.wait_ge(pad_in, 48)
            sp.dma_start(dst_raw[:, :], bass.AP(dst_pad, 0, [[TILES, P], [1, TILES + 2]])).then_inc(edges_in, 16)
            for tile, w in ((wq, Wq), (wk, Wk), (wv, Wv), (wo, Wo), (w1, W1)):
                sp.dma_start(tile[:, :], w).then_inc(consts_in, 16)
            for c, b in enumerate((bq, bk, bv)):
                sp.dma_start(bcol[:, c:c + 1], b.rearrange("(p a) -> p a", a=1)).then_inc(consts_in, 16)
            sp.dma_start(bb_col[:, :], bb.rearrange("(p a) -> p a", a=1).to_broadcast([P, 1])).then_inc(consts_in, 16)
            sp.dma_start(wb_row[:, :], Wb.rearrange("e a -> a e").to_broadcast([P, ED])).then_inc(consts_in, 16)
            sp.dma_start(bo_row[:, :], bo.rearrange("(a d) -> a d", a=1).to_broadcast([P, D])).then_inc(consts_in, 16)
            for t in range(G):
                sp.dma_start(bo_group[:, t * D:(t + 1) * D], bo.rearrange("(a d) -> a d", a=1)).then_inc(consts_in, 16)
            for c in range(2):
                sp.dma_start(a_col[:, c:c + 1], a1[c * D:(c + 1) * D, :]).then_inc(consts_in, 16)
            ev = edge_attr[0:head * TILES, :].rearrange("(p t) e -> p (t e)", p=head)
            sp.dma_start(edge_in[0:head, :], ev).then_inc(attr_in, 16)
            sp.dma_start(edge_in[head:P - 1, :], edge_attr[head * TILES:(P - 1) * TILES, :]
                         .rearrange("(p t) e -> p (t e)", t=TILES)).then_inc(attr_in, 16)
            sp.dma_start(edge_in[P - 1:P, 0:LASTROW * ED], edge_attr[(P - 1) * TILES:NE, :]
                         .rearrange("(p t) e -> p (t e)", p=1)).then_inc(attr_in, 16)

            def stage2(s):
                if s.runs(GROUPS):
                    wait(sp, node_applied, s.g - 1)
                    sp.dma_start(node_in[0:chunk_parts(s), s.u, :], node_chunk(x, s)).then_inc(node_loaded[s.u], 16)
                b = s.back(1)
                if b.runs(GROUPS):
                    wait(sp, got_dst[b.u], b.uses * 16 * G)
                    sp.dma_start(edge_view(xd_rows)[:, bass.ds(b.g * GW, GW)], xd[:, b.u, :]).then_inc(xd_stored[b.u], 16)
                b = s.back(2)
                if b.runs(GROUPS):
                    n = chunk_parts(b)
                    wait(sp, node_applied, b.g + 1)
                    sp.dma_start(node_chunk(x1_table, b), node_x1[0:n, b.u, :]).then_inc(x1_stored[b.u], 16)
                    sp.dma_start(node_chunk(out, b), node_out[0:n, b.u, :]).then_inc(out_stored[b.u], 16)
            pipeline(sp, stage2, 2)

            for u in range(2):
                sp.wait_ge(xd_stored[u], SLOTS_TOTAL[u])

            def stage4(s):
                if s.runs(GROUPS):
                    wait(sp, vx_T, s.g - 1)
                    wait(sp, c_y, s.g - 1)
                    sp.dma_start(xd[:, s.u, :], edge_view(xd_rows)[:, bass.ds(s.g * GW, GW)]).then_inc(xd_back[s.u], 16)
                b = s.back(3)
                if b.runs(GROUPS):
                    wait(sp, c_applied, b.g + 1)
                    sp.dma_start(edge_view(x1d_rows)[:, bass.ds(b.g * GW, GW)], res[:, b.u, :]).then_inc(x1d_stored[b.u], 16)
            pipeline(sp, stage4, 3)

            def stage5(s):
                wait(sp, d_got[s.u], s.uses * 16 * G)
                sp.dma_start(edge_view(xs_rows)[:, bass.ds(s.g * GW, GW)], xs[:, s.u, :]).then_inc(xs_stored[s.u], 16)
            pipeline(sp, stage5)

            for u in range(2):
                sp.wait_ge(xs_stored[u], SLOTS_TOTAL[u])
                sp.wait_ge(x1d_stored[u], SLOTS_TOTAL[u])

            def stage7(s):
                if s.runs(GROUPS):
                    if s.i is None and s.off < 2:
                        sp.wait_ge(d_done, GROUPS)
                    wait(sp, xa_done, s.g - 1)
                    sp.dma_start(xs[:, s.u, :], edge_view(xs_rows)[:, bass.ds(s.g * GW, GW)]).then_inc(xs_back[s.u], 16)
                b = s.back(1)
                if b.runs(GROUPS):
                    wait(sp, e_y, b.g - 1)
                    sp.dma_start(xd[:, b.u, :], edge_view(x1d_rows)[:, bass.ds(b.g * GW, GW)]).then_inc(x1d_back[b.u], 16)
            pipeline(sp, stage7, 1)
            for u in range(2):
                sp.wait_ge(out_stored[u], SLOTS_TOTAL[u])
                sp.wait_ge(e_scat[u], SLOTS_TOTAL[u] * G)
            sp.wait_ge(f_scat, 16)

        @block.gpsimd
        def _(pool):
            pool.memset(sentinel[:, :], N).then_inc(built, 1)
            pool.wait_ge(built, 1)
            pool.memset(sentinel[:, 0:1], -1).then_inc(zeroed, 1)
            pool.memset(src_tab[:, :], 0)
            pool.memset(edge_in[:, LASTROW * ED:TILES * ED], 0.0).then_inc(zeroed, 1)
            pool.memset(ident[:, :], 0.0)
            pool.memset(expand[:, :, :], 0.0)
            pool.memset(head_sel[:, :], 1.0).then_inc(built, 1)
            pool.wait_ge(built, 2)
            pool.affine_select(out=ident[:, :], in_=ident[:, :], compare_op=ALU.not_equal, fill=1.0,
                               base=0, pattern=[[-1, P]], channel_multiplier=1)
            ex = expand[:, :, :].rearrange("q t (h c) -> q t h c", h=H)
            pool.affine_select(out=ex, in_=ex, compare_op=ALU.not_equal, fill=1.0,
                               base=0, pattern=[[-H, G], [-1, H], [0, HD]], channel_multiplier=1)
            pool.affine_select(out=head_sel[:, :], in_=head_sel[:, :], compare_op=ALU.is_ge, fill=0.0,
                               base=0, pattern=[[-HD, H]], channel_multiplier=1).then_inc(built, 1)
            pool.wait_ge(built, 3)
            pool.affine_select(out=head_sel[:, :], in_=head_sel[:, :], compare_op=ALU.is_ge, fill=0.0,
                               base=HD - 1, pattern=[[HD, H]], channel_multiplier=-1).then_inc(built, 1)

            def rows(tile, u, t):
                return tile[:, u, t * D:(t + 1) * D]

            def gather(tile, table, idx, u, t, done):
                pool.indirect_dma_start(out=rows(tile, u, t), out_offset=None, in_=table,
                                        in_offset=bass.IndirectOffsetOnAxis(ap=idx, axis=0))\
                    .then_inc(done, 16)

            def scatter(table, tile, idx, u, t, done):
                pool.indirect_dma_start(out=table, out_offset=bass.IndirectOffsetOnAxis(ap=idx, axis=0),
                                        in_=rows(tile, u, t), in_offset=None,
                                        bounds_check=N - 1, oob_is_err=False).then_inc(done, 16)

            def stage2(s):
                hold(pool, idx_ready, s.g + 1)
                hold(pool, xT_done, s.g - 1)
                for t in range(G):
                    gather(xs, x, idx_slot[:, s.u, t:t + 1], s.u, t, got_src[s.u])
                prior = s.back(2)
                hold(pool, xd_stored[s.u], prior.uses * 16)
                for t in range(G):
                    gather(xd, x, idx_slot[:, s.u, G + t:G + t + 1], s.u, t, got_dst[s.u])
            pipeline(pool, stage2)

            for u in range(2):
                pool.wait_ge(x1_stored[u], SLOTS_TOTAL[u])

            def stage4(s):
                hold(pool, c_applied, s.g + 1)
                for t in range(G):
                    scatter(x1_table, res, idx_slot[:, s.u, t:t + 1], s.u, t, c_scat[s.u])
            pipeline(pool, stage4)
            for u in range(2):
                pool.wait_ge(c_scat[u], SLOTS_TOTAL[u] * G)

            def stage5(s):
                hold(pool, d_idx, s.g + 1)
                hold(pool, d_done, s.g - 1)
                prior = s.back(2)
                hold(pool, xs_stored[s.u], prior.uses * 16)
                for t in range(G):
                    gather(xs, x1_table, idx_slot[:, s.u, t:t + 1], s.u, t, d_got[s.u])
            pipeline(pool, stage5)
            gather_c = pool.indirect_dma_start(out=x1c[:, :], out_offset=None, in_=x1_table,
                                               in_offset=bass.IndirectOffsetOnAxis(ap=carry_idx[:, 0:1], axis=0))
            gather_c.then_inc(f_got, 16)
            for u in range(2):
                pool.wait_ge(out_stored[u], SLOTS_TOTAL[u])

            def stage7(s):
                hold(pool, e_applied, s.g + 1)
                for t in range(G):
                    scatter(out, res, idx_slot[:, s.u, t:t + 1], s.u, t, e_scat[s.u])
            pipeline(pool, stage7)
            pool.wait_ge(f_act, 3)
            pool.indirect_dma_start(out=out, out_offset=bass.IndirectOffsetOnAxis(ap=carry_idx[:, 1:2], axis=0),
                                    in_=total[:, :], in_offset=None,
                                    bounds_check=N - 1, oob_is_err=False).then_inc(f_scat, 16)

        @block.tensor
        def _(pe):
            mm, tr = nc.tensor.matmul, nc.tensor.transpose
            pe.wait_ge(consts_in, 16 * 17)
            pe.wait_ge(built, 4)
            tr(bank[0][:, 0:P], w1[:, :], ident[:, :]).then_inc(w1T_done, 1)
            pe.wait_ge(w1T_sb, 1)
            pe.wait_ge(prep, 1)
            for c in range(2):
                last = mm(bank[1][:, c * D:(c + 1) * D], a_wide[:, c, :], w1T[:, :], start=True, stop=True)
            last.then_inc(v_done, 1)

            def stage2(s):
                wait(pe, got_src[s.u], s.uses * 16 * G)
                wait(pe, got_dst[s.u], s.uses * 16 * G)
                wait(pe, xT_sb, s.g * 2)
                for t in range(G):
                    tr(bank[2][:, t * P:(t + 1) * P], T(xs, s.u, t), ident[:, :])
                for t in range(G):
                    last = tr(bank[3][:, t * P:(t + 1) * P], T(xd, s.u, t), ident[:, :])
                last.then_inc(xT_done, 1)
                wait(pe, xT_sb, s.g * 2 + 2)
                wait(pe, q_sb, s.g)
                wait(pe, prod_done, s.g)
                mm(bank[4][:, :], wq[:, :], xsT[:, :], start=True, stop=True)
                mm(bank[5][:, :], wk[:, :], xdT[:, 0, :], start=True, stop=True).then_inc(qk_done, 1)
                wait(pe, prod_done, s.g + 1)
                wait(pe, score_done, s.g)
                for t in range(G):
                    last = mm(bank[6][:, t * H:(t + 1) * H], prodT[:, t * P:(t + 1) * P], head_sel[:, :],
                              start=True, stop=True)
                last.then_inc(s_done, 1)
            pe.wait_ge(prep, 2)
            pipeline(pe, stage2)

            for k in range(2):
                pe.wait_ge(ends_ready, k + 1)
                tr(bank[0][0:H, 0:P], ends[:, 0, :], ident[:, :])
                tr(bank[0][0:H, P:2 * P], ends[:, 1, :], ident[:, :]).then_inc(ends_T, 1)
                pe.wait_ge(row_ready, k + 1)
                tr(bank[1][:, 0:H], carry_row[:, k, 0:P], ident[0:H, 0:H]).then_inc(carry_T, 1)

            def stage4(s):
                if s.runs(GROUPS):
                    wait(pe, xd_back[s.u], s.uses * 16)
                    wait(pe, vx_Tsb, s.g)
                    for t in range(G):
                        last = tr(bank[2][:, t * P:(t + 1) * P], T(xd, s.u, t), ident[:, :])
                    last.then_inc(vx_T, 1)
                    wait(pe, share_cp, s.g + 1)
                    wait(pe, shT_sb, s.g)
                    tr(bank[3][0:G * H, 0:P], share_slot[:, s.u, :], ident[:, :]).then_inc(shT, 1)
                    wait(pe, vx_Tsb, s.g + 1)
                    wait(pe, v_sb, s.g - 1)
                    mm(bank[4 + s.u][:, :], wv[:, :], xdT[:, s.u, :], start=True, stop=True).then_inc(v_mm, 1)
                    wait(pe, shT_sb, s.g + 1)
                    wait(pe, h_done, s.g - 1)
                    for t in range(G):
                        last = mm(bank[6 + s.u][:, t * P:(t + 1) * P], expand[:, t, :], shareT[:, s.u, :],
                                  start=True, stop=True)
                    last.then_inc(x_mm, 1)
                b = s.back(1)
                if b.runs(GROUPS):
                    wait(pe, h_done, b.g + 1)
                    wait(pe, c_y, b.g - 1)
                    o = bank[b.u]
                    for t in range(G):
                        mm(o[:, t * D:(t + 1) * D], T(hT, b.u, t), wo[:, :], start=True, stop=False)
                        last = mm(o[:, t * D:(t + 1) * D], ones[0:1, :], bo_group[:, t * D:(t + 1) * D],
                                  start=False, stop=True)
                    last.then_inc(o_mm, 1)
            pe.wait_ge(share_done, 1)
            pipeline(pe, stage4, 1)

            pe.wait_ge(max_col, 1)
            tr(bank[2][0:1, 0:P], max_p[:, :], ident[:, :]).then_inc(max_T, 1)
            pe.wait_ge(max_one, 1)
            mm(bank[3][:, 0:1], ones[0:1, :], max_all[:, :], start=True, stop=True).then_inc(max_b, 1)
            pe.wait_ge(exp_done, 1)
            mm(bank[4][:, 0:1], ones[:, :], exp_sum[:, :], start=True, stop=True)
            mm(bank[5][:, 0:P], ones[:, :], diag[:, :], start=True, stop=True).then_inc(sum_b, 1)
            pe.wait_ge(att_ready, 1)

            def stage7(s):
                if s.runs(GROUPS):
                    wait(pe, r_done, s.g + 1)
                    wait(pe, e_Tsb, s.g - 1)
                    for t in range(G):
                        last = tr(bank[2 + s.u][:, t * P:(t + 1) * P], T(agg, s.u, t), ident[:, :])
                    last.then_inc(e_T, 1)
                b = s.back(1)
                if b.runs(GROUPS):
                    wait(pe, e_Tsb, b.g + 1)
                    wait(pe, e_y, b.g - 1)
                    for t in range(G):
                        last = mm(bank[b.u][:, t * D:(t + 1) * D], T(aggT, b.u, t), w1[:, :], start=True, stop=True)
                    last.then_inc(e_mm, 1)
            pipeline(pe, stage7, 1)
            tr(bank[4][:, 0:P], T(agg, (GROUPS - 1) % 2, G - 1), ident[:, :]).then_inc(f_pe, 1)
            pe.wait_ge(f_dve, 1)
            tr(bank[5][:, 0:P], carryT[:, 0:P], ident[:, :]).then_inc(f_pe, 1)
            pe.wait_ge(f_dve, 2)
            tr(bank[6][:, 0:P], total[:, :], ident[:, :]).then_inc(f_pe, 1)
            pe.wait_ge(f_act, 1)
            mm(bank[7][:, 0:D], totalT[:, :], w1[:, :], start=True, stop=True).then_inc(f_pe, 1)

        @block.scalar
        def _(act):
            fn = nc.scalar.activation
            act.wait_ge(w1T_done, 1)
            fn(w1T[:, :], bank[0][:, 0:P], ACT.Copy).then_inc(w1T_sb, 1)

            def stage2(s):
                if s.runs(GROUPS):
                    wait(act, xT_done, s.g + 1)
                    wait(act, qk_done, s.g)
                    fn(xsT[:, :], bank[2][:, :], ACT.Copy).then_inc(xT_sb, 1)
                    fn(xdT[:, 0, :], bank[3][:, :], ACT.Copy).then_inc(xT_sb, 1)
                    wait(act, qk_done, s.g + 1)
                    wait(act, prod_done, s.g)
                    fn(qT[:, :], bank[4][:, :], ACT.Identity, bias=bcol[:, 0:1]).then_inc(q_sb, 1)
                if s.runs(GROUPS):
                    n = chunk_parts(s)
                    wait(act, node_var, s.g + 1)
                    wait(act, node_ready, s.g - 1)
                    var = nmv[0:n, s.u, :, 1]
                    fn(nstd[0:n, s.u, 0, :], var, ACT.Sqrt, bias=eps_cols[0:n, 0:1])
                    fn(nstd[0:n, s.u, 1, :], var, ACT.Sqrt, bias=eps_cols[0:n, 1:2], scale=1.0 + EPS)\
                        .then_inc(node_std, 1)
                b = s.back(1)
                if b.runs(GROUPS):
                    n = chunk_parts(b)
                    prior = b.back(2)
                    wait(act, node_ready, b.g + 1)
                    wait(act, x1_stored[b.u], prior.uses * 16)
                    wait(act, out_stored[b.u], prior.uses * 16)
                    for r in range(ROWS):
                        cols = slice(r * D, (r + 1) * D)
                        for k, to in enumerate((node_x1, node_out)):
                            last = fn(to[0:n, b.u, cols], node_in[0:n, b.u, cols], ACT.Identity,
                                      bias=nsc[0:n, b.u, 1, k, r:r + 1], scale=nsc[0:n, b.u, 0, k, r:r + 1])
                    last.then_inc(node_applied, 1)
            act.wait_ge(consts_in, 16 * 17)
            pipeline(act, stage2, 1)

            for k in range(3):
                act.wait_ge(args_ready, k + 1)
                e = (weight, decay, tmp)[k]
                fn(e[:, :, :], e[:, :, :], ACT.Exp).then_inc(exps_done, 1)
            act.wait_ge(share_done, 1)

            def apply(b, stats, done, at, first_free):
                wait(act, stats, b.g + 1)
                first_free()
                fn(idx_slot[:, b.u, 0:G], at[:, bass.ds(b.g * G, G)], ACT.Copy)
                for t in range(G):
                    last = fn(T(res, b.u, t), T(y, b.u, t), ACT.Identity,
                              bias=ysc[:, b.u, 1, t:t + 1], scale=ysc[:, b.u, 0, t:t + 1])
                last.then_inc(done, 1)

            def deviation(b, var_ready, std_ready, stats):
                wait(act, var_ready, b.g + 1)
                wait(act, stats, b.g - 1)
                fn(ystd[:, b.u, :], ymv[:, b.u, :, 1], ACT.Sqrt, bias=eps_cols[:, 0:1]).then_inc(std_ready, 1)

            def stage4(s):
                if s.runs(GROUPS):
                    wait(act, shT, s.g - 1)
                    fn(share_slot[:, s.u, :], share[:, bass.ds(s.g * G, G), :], ACT.Copy).then_inc(share_cp, 1)
                    wait(act, vx_T, s.g + 1)
                    wait(act, v_mm, s.g - 1)
                    fn(xdT[:, s.u, :], bank[2][:, :], ACT.Copy).then_inc(vx_Tsb, 1)
                    wait(act, shT, s.g + 1)
                    wait(act, x_mm, s.g - 1)
                    fn(shareT[:, s.u, :], bank[3][0:G * H, 0:P], ACT.Copy).then_inc(shT_sb, 1)
                    wait(act, v_mm, s.g + 1)
                    wait(act, h_done, s.g - 1)
                    fn(vT[:, s.u, :], bank[4 + s.u][:, :], ACT.Identity, bias=bcol[:, 2:3]).then_inc(v_sb, 1)
                b = s.back(2)
                if b.runs(GROUPS):
                    def free():
                        prior = b.back(2)
                        wait(act, sd_done, b.g - 1)
                        wait(act, x1d_stored[b.u], prior.uses * 16)
                        wait(act, c_scat[b.u], prior.uses * 16 * G)
                    apply(b, c_stats, c_applied, at_last, free)
                b = s.back(1)
                if b.runs(GROUPS):
                    deviation(b, c_var, c_std, c_stats)
            pipeline(act, stage4, 2)

            act.wait_ge(neg_ready, 1)
            fn(att[:, :], logit[:, :], ACT.Exp, bias=neg_max[:, :], accum_out=exp_sum[:, :]).then_inc(exp_done, 1)
            act.wait_ge(att_ready, 1)
            for u in range(2):
                act.wait_ge(x1d_stored[u], SLOTS_TOTAL[u])
                act.wait_ge(c_scat[u], SLOTS_TOTAL[u] * G)

            def stage7(s):
                if s.runs(GROUPS):
                    wait(act, xs_back[s.u], s.uses * 16)
                    wait(act, r_done, s.g - 1)
                    for t in range(G):
                        last = fn(T(xa, s.u, t), T(xs, s.u, t), ACT.Copy, scale=att[:, bass.ds(s.g * G + t, 1)])
                    last.then_inc(xa_done, 1)
                b = s.back(1)
                if b.runs(GROUPS):
                    wait(act, e_T, b.g + 1)
                    wait(act, e_mm, b.g - 1)
                    fn(aggT[:, b.u, :], bank[2 + b.u][:, :], ACT.Copy).then_inc(e_Tsb, 1)
                c = s.back(3)
                if c.runs(GROUPS):
                    apply(c, e_stats, e_applied, at_last2,
                          lambda: wait(act, e_scat[c.u], c.back(2).uses * 16 * G))
                c = s.back(2)
                if c.runs(GROUPS):
                    deviation(c, e_var, e_std, e_stats)
            pipeline(act, stage7, 3)
            act.wait_ge(f_pe, 3)
            fn(totalT[:, :], bank[6][:, 0:P], ACT.Copy).then_inc(f_act, 1)
            act.wait_ge(f_dve, 3)
            fn(ystd[:, 0, 0:1], ymv[:, 0, 0, 1:2], ACT.Sqrt, bias=eps_cols[:, 0:1]).then_inc(f_act, 1)
            act.wait_ge(f_dve, 4)
            fn(total[:, :], y[:, 0, 0:D], ACT.Identity, bias=ysc[:, 0, 1, 0:1], scale=ysc[:, 0, 0, 0:1])\
                .then_inc(f_act, 1)

        @block.vector
        def _(dve):
            v = nc.vector
            chain = Chain(dve, prep_chain, None)
            v.memset(ones[:, :], 1.0)
            v.memset(eps_cols[:, 0:1], EPS)
            v.memset(eps_cols[:, 1:2], EPS * EPS)
            v.memset(dst_tab[:, TILES:], 0)
            v.memset(agg[:, 1, :], 0.0)
            v.memset(part[:, :], 0.0)
            v.memset(carryT[:, 0:1], 0.0)
            v.memset(carry_row[:, 0, 0:1], -BIG)
            v.memset(decay[:, :, 0:1], -BIG)
            v.memset(carry_row[:, 1, 0:1], 0.0)
            dve.wait_ge(consts_in, 16 * 17)
            for c in range(2):
                last = v.tensor_copy(a_wide[:, c, :], a_col[:, c:c + 1].to_broadcast([P, P]))
            last.then_inc(prep, 1)
            dve.wait_ge(edges_in, 16)
            chain.link(v.tensor_copy(dst_f[:, :], dst_raw[:, :]))
            cur, prv, nxt = dst_f[:, 1:TILES + 1], dst_f[:, 0:TILES], dst_f[:, 2:TILES + 2]
            v.tensor_scalar(dst_cl[:, :], cur, float(N - 1), None, ALU.min)
            v.tensor_tensor(same_prev[:, :], cur, prv, ALU.is_equal)
            v.tensor_tensor(same_next[:, :], cur, nxt, ALU.is_equal)
            v.tensor_scalar(pen_pad[:, :], cur, float(N), -BIG, ALU.is_ge, ALU.mult)
            chain.link(v.tensor_scalar(first[:, :], cur, dst_f[:, 0:1], None, ALU.is_equal))
            v.tensor_copy(dst_tab[:, 0:TILES], dst_cl[:, :])
            v.memset(same_prev[:, 0:1], 0.0)
            v.scalar_tensor_tensor(at_last_f[:, :], same_next[:, :], SKIP, cur, ALU.mult, ALU.add)
            v.tensor_scalar(pen_first[:, :], first[:, :], 1.0, BIG, ALU.subtract, ALU.mult)
            v.tensor_tensor(first_last[:, :], first[:, :], same_next[:, :], ALU.mult)
            v.tensor_scalar(carry_idx_f[:, 0:1], dst_f[:, 0:1], 0.0, float(N - 1), ALU.max, ALU.min)
            v.tensor_tensor(carry_idx_f[:, 2:3], dst_f[:, TILES + 1:TILES + 2], dst_f[:, 0:1], ALU.is_equal)
            dve.wait_ge(built, 4)
            chain.link(v.tensor_scalar(diag[:, :], ident[:, :], first[:, TILES - 1:TILES], None, ALU.mult))
            v.tensor_tensor(first_last[:, :], first[:, :], first_last[:, :], ALU.subtract)
            v.tensor_copy(at_last[:, 0:TILES], at_last_f[:, :])
            v.scalar_tensor_tensor(at_last2_f[:, :], first[:, :], SKIP, at_last_f[:, :], ALU.mult, ALU.add)
            v.tensor_copy(carry_idx[:, 0:1], carry_idx_f[:, 0:1])
            chain.link(v.tensor_tensor(carry_idx_f[:, 3:4], carry_idx_f[:, 2:3], first[:, 0:1], ALU.subtract))
            v.tensor_copy(at_last2[:, 0:TILES], at_last2_f[:, :])
            chain.link(v.tensor_scalar(carry_idx_f[:, 2:3], carry_idx_f[:, 3:4], 1.0, SKIP, ALU.add, ALU.mult))
            chain.link(v.tensor_tensor(carry_idx_f[:, 3:4], carry_idx_f[:, 2:3], dst_f[:, 0:1], ALU.add))
            v.tensor_copy(carry_idx[:, 1:2], carry_idx_f[:, 3:4])
            v.tensor_copy(ends[:, 1, :], pen_first[:, TILES - 1:TILES].to_broadcast([P, H]))
            v.tensor_scalar(pen_local[:, :, :], same_prev[:, :].unsqueeze(1).to_broadcast([P, H, TILES]),
                            1.0, BIG, ALU.subtract, ALU.mult)
            dve.wait_ge(src_in, 48)
            dve.wait_ge(v_done, 1)
            v.tensor_copy(v_src[:, :], bank[1][:, 0:D])
            v.tensor_copy(v_dst[:, :], bank[1][:, D:2 * D]).then_inc(prep, 1)

            def fetch_indices(s, both, ready):
                at = bass.ds((s.g + 2) * G, G)
                last = v.tensor_copy(idx_slot[:, s.u, 0:G], src_tab[:, at])
                if both:
                    last = v.tensor_copy(idx_slot[:, s.u, G:2 * G], dst_tab[:, at])
                last.then_inc(ready, 1)

            def stage2(s):
                if s.runs(GROUPS):
                    c = Chain(dve, bias_chain, 3, s)
                    cols = bass.ds(s.g * G * ED, G * ED)
                    mul = edge_mul[:, :].rearrange("p (t e) -> p t e", t=G)
                    c.link(v.tensor_tensor(mul, edge_in[:, cols].rearrange("p (t e) -> p t e", t=G),
                                           wb_row[:, :].unsqueeze(1).to_broadcast([P, G, ED]), ALU.mult))
                    c.link(v.tensor_reduce(edge_bias[:, 0, :], mul, AX, ALU.add))
                    c.link(v.tensor_scalar(edge_bias[:, 1, :], edge_bias[:, 0, :], bb_col[:, :], None, ALU.add))
                    n = chunk_parts(s)
                    c = Chain(dve, node_chain, 2, s)
                    yv = node_in[0:n, s.u, :].rearrange("p (r d) -> p r d", r=ROWS)
                    wait(dve, node_loaded[s.u], s.uses * 16)
                    c.link(v.tensor_tensor(yv, yv, bo_row[0:n, :].unsqueeze(1).to_broadcast([n, ROWS, D]), ALU.add))
                    for r in range(ROWS):
                        last = v.bn_stats(nst[0:n, r, :], node_in[0:n, s.u, r * D:(r + 1) * D])
                    c.link(last)
                    for r in range(ROWS):
                        last = v.bn_aggr(nmv[0:n, s.u, r, :], nst[0:n, r, :])
                    last.then_inc(node_var, 1)
                b = s.back(1)
                if b.runs(GROUPS):
                    n = chunk_parts(b)
                    c = Chain(dve, node_fin_chain, 1, b)
                    wait(dve, node_std, b.g + 1)
                    wait(dve, node_applied, b.g - 1)
                    c.link(v.reciprocal(nsc[0:n, b.u, 0, :, :], nstd[0:n, b.u, :, :]))
                    v.scalar_tensor_tensor(nsc[0:n, b.u, 1, :, :],
                                           nmv[0:n, b.u, :, 0].unsqueeze(1).to_broadcast([n, 2, ROWS]), -1.0,
                                           nsc[0:n, b.u, 0, :, :], ALU.mult, ALU.mult).then_inc(node_ready, 1)
                if s.runs(GROUPS):
                    wait(dve, q_sb, s.g + 1)
                    wait(dve, s_done, s.g)
                    v.scalar_tensor_tensor(prodT[:, :], bank[5][:, :], bcol[:, 1:2], qT[:, :], ALU.add, ALU.mult)\
                        .then_inc(prod_done, 1)
                    fetch_indices(s, True, idx_ready)
                    wait(dve, s_done, s.g + 1)
                    v.scalar_tensor_tensor(score[:, :, bass.ds(s.g * G, G)],
                                           bank[6][:, 0:G * H].rearrange("p (t h) -> p h t", t=G),
                                           float(HD) ** -0.5,
                                           edge_bias[:, 1, :].unsqueeze(1).to_broadcast([P, H, G]),
                                           ALU.mult, ALU.add).then_inc(score_done, 1)
            fetch_indices(Step(-2), True, idx_ready)
            fetch_indices(Step(-1), True, idx_ready)
            dve.wait_ge(attr_in, 48)
            pipeline(dve, stage2, 1)

            flat = lambda a: a[:, :, :].rearrange("p h t -> p (h t)")
            along = lambda a: a.unsqueeze(1).to_broadcast([P, H, TILES])
            over = lambda a: a.unsqueeze(2).to_broadcast([P, H, TILES])
            c = Chain(dve, soft_chain, None)
            dve.wait_ge(score_done, GROUPS)
            c.link(v.tensor_tensor_scan(flat(run_max), flat(pen_local), flat(score), -BIG, ALU.add, ALU.max))
            v.tensor_copy(ends[:, 0, :], run_max[:, :, TILES - 1]).then_inc(ends_ready, 1)
            dve.wait_ge(ends_T, 1)
            c.link(v.tensor_copy(factor_row[:, :], bank[0][0:H, P:2 * P]))
            v.tensor_tensor_scan(carry_row[:, 0, 1:P + 1], factor_row[:, :], bank[0][0:H, 0:P], -BIG,
                                 ALU.add, ALU.max).then_inc(row_ready, 1)
            dve.wait_ge(carry_T, 1)
            c.link(v.tensor_copy(carry_in[:, :], bank[1][:, 0:H]))
            c.link(v.tensor_tensor(tmp[:, :, :], along(pen_first[:, :]), over(carry_in[:, :]), ALU.add))
            c.link(v.tensor_tensor(run_max[:, :, :], run_max[:, :, :], tmp[:, :, :], ALU.max))
            v.tensor_tensor(weight[:, :, :], score[:, :, :], run_max[:, :, :], ALU.subtract).then_inc(args_ready, 1)
            c.link(v.tensor_tensor(decay[:, :, 1:TILES], run_max[:, :, 0:TILES - 1], run_max[:, :, 1:TILES],
                                   ALU.subtract))
            v.tensor_tensor(decay[:, :, 1:TILES], decay[:, :, 1:TILES], pen_local[:, :, 1:TILES], ALU.add)\
                .then_inc(args_ready, 1)
            v.tensor_tensor(tmp[:, :, :], tmp[:, :, :], run_max[:, :, :], ALU.subtract).then_inc(args_ready, 1)
            dve.wait_ge(exps_done, 3)
            c.link(v.tensor_tensor_scan(flat(run_sum), flat(decay), flat(weight), 0.0, ALU.mult, ALU.add))
            v.tensor_copy(ends[:, 1, :], tmp[:, :, TILES - 1])
            v.tensor_copy(ends[:, 0, :], run_sum[:, :, TILES - 1]).then_inc(ends_ready, 1)
            dve.wait_ge(ends_T, 2)
            c.link(v.tensor_copy(factor_row[:, :], bank[0][0:H, P:2 * P]))
            v.tensor_tensor_scan(carry_row[:, 1, 1:P + 1], factor_row[:, :], bank[0][0:H, 0:P], 0.0,
                                 ALU.mult, ALU.add).then_inc(row_ready, 1)
            dve.wait_ge(carry_T, 2)
            c.link(v.tensor_copy(carry_in[:, :], bank[1][:, 0:H]))
            c.link(v.tensor_tensor(tmp[:, :, :], tmp[:, :, :], over(carry_in[:, :]), ALU.mult))
            c.link(v.tensor_tensor(run_sum[:, :, :], run_sum[:, :, :], tmp[:, :, :], ALU.add))
            c.link(v.reciprocal(decay[:, :, :], run_sum[:, :, :]))
            v.tensor_tensor(share[:, :, :].rearrange("p t h -> p h t"), run_sum[:, :, :], decay[:, :, :], ALU.mult)\
                .then_inc(share_done, 1)

            def tail(b, o_ready, y_done, chain_sem, var_ready, applied):
                c = Chain(dve, chain_sem, 1, b)
                wait(dve, o_ready, b.g + 1)
                wait(dve, applied, b.g - 1)
                v.tensor_tensor(y[:, b.u, :], xd[:, b.u, :], bank[b.u][:, :], ALU.add).then_inc(y_done, 1)
                wait(dve, y_done, b.g + 1)
                for t in range(G):
                    last = v.bn_stats(yst[:, t, :], T(y, b.u, t))
                c.link(last)
                for t in range(G):
                    last = v.bn_aggr(ymv[:, b.u, t, :], yst[:, t, :])
                last.then_inc(var_ready, 1)

            def finish(b, chain_sem, std_ready, stats_done, applied):
                c = Chain(dve, chain_sem, 1, b)
                wait(dve, std_ready, b.g + 1)
                wait(dve, applied, b.g - 1)
                c.link(v.reciprocal(ysc[:, b.u, 0, :], ystd[:, b.u, :]))
                v.scalar_tensor_tensor(ysc[:, b.u, 1, :], ymv[:, b.u, :, 0], -1.0, ysc[:, b.u, 0, :],
                                       ALU.mult, ALU.mult).then_inc(stats_done, 1)

            def dot(rows, vector, scores, b, chain_sem, done):
                c = Chain(dve, chain_sem, 1, b)
                wait(dve, done, b.g)
                wide = lambda a: a.rearrange("p (t d) -> p t d", t=G)
                c.link(v.tensor_tensor(wide(dots[:, :]), wide(rows[:, b.u, :]),
                                       vector[:, :].unsqueeze(1).to_broadcast([P, G, D]), ALU.mult))
                v.tensor_reduce(scores[:, bass.ds(b.g * G, G)], wide(dots[:, :]), AX, ALU.add).then_inc(done, 1)

            def stage4(s):
                if s.runs(GROUPS):
                    wait(dve, v_sb, s.g + 1)
                    wait(dve, x_mm, s.g + 1)
                    wait(dve, o_mm, s.g - 1)
                    v.tensor_tensor(hT[:, s.u, :], vT[:, s.u, :], bank[6 + s.u][:, :], ALU.mult).then_inc(h_done, 1)
                d = s.back(2)
                if d.runs(GROUPS):
                    finish(d, c_fin_chain, c_std, c_stats, c_applied)
                d = s.back(3)
                if d.runs(GROUPS):
                    wait(dve, c_applied, d.g + 1)
                    dot(res, v_dst, s_dst, d, sd_chain, sd_done)
                b = s.back(1)
                if b.runs(GROUPS):
                    tail(b, o_mm, c_y, c_chain, c_var, c_applied)
            pipeline(dve, stage4, 3)

            for u in range(2):
                dve.wait_ge(c_scat[u], SLOTS_TOTAL[u] * G)
            fetch_indices(Step(-2), False, d_idx)
            fetch_indices(Step(-1), False, d_idx)

            def stage5(s):
                wait(dve, d_got[s.u], s.uses * 16 * G)
                fetch_indices(s, False, d_idx)
                dot(xs, v_src, s_src, s, d_chain, d_done)
            pipeline(dve, stage5)

            c = Chain(dve, att_chain, None)
            dve.wait_ge(d_done, GROUPS)
            c.link(v.tensor_tensor(logit[:, :], s_src[:, :], s_dst[:, :], ALU.add))
            c.link(v.scalar_tensor_tensor(logit2[:, :], logit[:, :], SLOPE, logit[:, :], ALU.mult, ALU.max))
            c.link(v.tensor_tensor(logit[:, :], logit2[:, :], pen_pad[:, :], ALU.add))
            v.tensor_reduce(max_p[:, :], logit[:, :], AX, ALU.max).then_inc(max_col, 1)
            dve.wait_ge(max_T, 1)
            v.tensor_reduce(max_all[:, :], bank[2][0:1, 0:P], AX, ALU.max).then_inc(max_one, 1)
            dve.wait_ge(max_b, 1)
            v.tensor_scalar(neg_max[:, :], bank[3][:, 0:1], -1.0, None, ALU.mult).then_inc(neg_ready, 1)
            dve.wait_ge(sum_b, 1)
            v.tensor_copy(chunkrow[:, :], bank[5][:, 0:P])
            c.link(v.reciprocal(inv_sum[:, :], bank[4][:, 0:1]))
            v.tensor_scalar(att[:, :], att[:, :], inv_sum[:, :], None, ALU.mult).then_inc(att_ready, 1)

            def stage7(s):
                if s.runs(GROUPS):
                    c = Chain(dve, r_chain, 7, s)
                    wait(dve, xa_done, s.g + 1)
                    wait(dve, e_T, s.g - 1)
                    col = lambda tab, t: tab[:, bass.ds(s.g * G + t, 1)]

                    def own(t):
                        return v.scalar_tensor_tensor(part[:, :], T(agg, s.u, t), col(first_last, t), part[:, :],
                                                      ALU.mult, ALU.add)
                    for t in range(G):
                        prev = T(agg, s.u, t - 1) if t else T(agg, 1 - s.u, G - 1)
                        ins = v.scalar_tensor_tensor(T(agg, s.u, t), prev, col(same_prev, t), T(xa, s.u, t),
                                                     ALU.mult, ALU.add)
                        if t == G - 1:
                            ins.then_inc(r_done, 1)
                            wait(dve, r_done, s.g + 1)
                        else:
                            c.link(ins)
                        if t:
                            c.link(own(t - 1))
                    c.link(own(G - 1))
                b = s.back(3)
                if b.runs(GROUPS):
                    finish(b, e_fin_chain, e_std, e_stats, e_applied)
                b = s.back(2)
                if b.runs(GROUPS):
                    wait(dve, x1d_back[b.u], b.uses * 16)
                    tail(b, e_mm, e_y, e_chain, e_var, e_applied)
            pipeline(dve, stage7, 3)

            c = Chain(dve, last_chain, None)
            dve.wait_ge(f_pe, 1)
            v.tensor_tensor_scan(carryT[:, 1:P + 1], chunkrow[:, :], bank[4][:, 0:P], 0.0, ALU.mult, ALU.add)\
                .then_inc(f_dve, 1)
            dve.wait_ge(f_pe, 2)
            v.tensor_tensor(total[:, :], part[:, :], bank[5][:, 0:P], ALU.add).then_inc(f_dve, 1)
            dve.wait_ge(f_pe, 4)
            dve.wait_ge(f_got, 16)
            dve.wait_ge(e_applied, GROUPS)
            c.link(v.tensor_tensor(y[:, 0, 0:D], x1c[:, :], bank[7][:, 0:D], ALU.add))
            c.link(v.bn_stats(yst[:, 0, :], y[:, 0, 0:D]))
            v.bn_aggr(ymv[:, 0, 0, :], yst[:, 0, :]).then_inc(f_dve, 1)
            dve.wait_ge(f_act, 2)
            c.link(v.reciprocal(ysc[:, 0, 0, 0:1], ystd[:, 0, 0:1]))
            v.scalar_tensor_tensor(ysc[:, 0, 1, 0:1], ymv[:, 0, 0, 0:1], -1.0, ysc[:, 0, 0, 0:1], ALU.mult, ALU.mult)\
                .then_inc(f_dve, 1)


_INS = ["x", "src", "dst", "edge_attr_64", "L0_gnn_Wq", "L0_gnn_bq", "L0_gnn_Wk", "L0_gnn_bk", "L0_gnn_Wv",
        "L0_gnn_bv", "L0_gnn_Wb", "L0_gnn_bb", "L0_gnn_Wo", "L0_gnn_bo", "L1_gnn_W", "L1_gnn_a"]


def kernel(**inputs):
    import numpy as np
    import concourse.bacc as bacc
    from concourse import mybir as mb
    from concourse.bass_utils import run_bass_kernel_spmd

    nc = bacc.Bacc("TRN2", target_bir_lowering=False, num_devices=1)
    arrays, args = {}, []
    for name in _INS:
        a = np.ascontiguousarray(inputs[name])
        arrays[f"in_{name}"] = a
        args.append(nc.dram_tensor(f"in_{name}", a.shape, mb.dt.from_np(a.dtype), kind="ExternalInput").ap())
    args.append(nc.dram_tensor("out_dram", inputs["x"].shape, mb.dt.float32, kind="ExternalOutput").ap())
    gnn_kernel(nc, *args)
    return run_bass_kernel_spmd(nc, [arrays], core_ids=[0]).results[0]["out_dram"]
```

```python
import concourse.bass as bass
from concourse import mybir
from contextlib import ExitStack


UNROLL = 4


class Step:

    def __init__(self, off, i=None):
        self.off, self.i = off, i
        self.u, self.w = off % 2, off % 4
        self.g = off if i is None else i * UNROLL + off

    def uses(self, ring):
        count = self.off // ring + 1
        return count if self.i is None else self.i * (UNROLL // ring) + count

    def back(self, k):
        return Step(self.off - k, self.i)

    def runs(self, groups):
        return self.i is not None or 0 <= self.off < groups


def gnn_kernel(nc, x, src, dst, edge_attr, Wq, bq, Wk, bk, Wv, bv, Wb, bb, Wo, bo, W1, a1, out):
    fp32 = mybir.dt.float32
    i32 = mybir.dt.int32
    ALU = mybir.AluOpType
    ACT = mybir.ActivationFunctionType
    AX = mybir.AxisListType.X

    P = 128
    N, D = x.shape
    NE = src.shape[0]
    ED = edge_attr.shape[1]
    H = 8
    HD = D // H
    G = 4
    TILES = -(-NE // (P * G)) * G
    GROUPS = TILES // G
    EP = P * TILES
    LASTROW = NE - (P - 1) * TILES
    ROWS = (N // P // (GROUPS - 1))
    MAIN = P * ROWS * (GROUPS - 1)
    REST = (N - MAIN) // ROWS
    PEEL = 9
    LOOPS = (GROUPS - PEEL) // UNROLL
    assert (GROUPS - PEEL) % UNROLL == 0 and REST * ROWS == N - MAIN and REST <= P and 0 < LASTROW <= TILES
    GW = G * D
    BW = ROWS * D
    EPS = 1e-5
    BIG = 1e30
    SKIP = 1e5
    SLOPE = 0.2
    CH = H * TILES

    xd_rows = nc.dram_tensor("xd_rows", (EP, D), fp32).ap()
    x1d_rows = nc.dram_tensor("x1d_rows", (EP, D), fp32).ap()
    xs_rows = nc.dram_tensor("xs_rows", (EP, D), fp32).ap()
    x1_table = nc.dram_tensor("x1_table", (N, D), fp32).ap()
    dst_pad = nc.dram_tensor("dst_pad", (EP + 2,), i32)

    def edge_view(a):
        return a.rearrange("(p t) d -> p (t d)", p=P)

    def node_chunk(a, s):
        if s.i is None and s.off == 0:
            return a[MAIN:N, :].rearrange("(p r) d -> p (r d)", r=ROWS)
        return a[0:MAIN, :].rearrange("(p k) d -> p (k d)", p=P)[:, bass.ds((s.g - 1) * BW, BW)]

    def chunk_parts(s):
        return REST if s.i is None and s.off == 0 else P

    with ExitStack() as ctx:
        def sb(name, shape, dt=fp32):
            return ctx.enter_context(nc.sbuf_tensor(name, shape, dt))

        def sem(name):
            return ctx.enter_context(nc.semaphore(name))

        def sems(name, ring):
            return [sem(f"{name}{u}") for u in range(ring)]

        bank = [ctx.enter_context(nc.psum_tensor(f"bank{i}", [P, 512], fp32)) for i in range(8)]

        ident = sb("ident", [P, P])
        ones = sb("ones", [P, P])
        head_sel = sb("head_sel", [P, H])
        expand = sb("expand", [G * H, G, D])
        wq, wk, wv, wo, w1, w1T = (sb(n, [P, D]) for n in ("wq", "wk", "wv", "wo", "w1", "w1T"))
        bcol = sb("bcol", [P, 3])
        bb_col = sb("bb_col", [P, 1])
        wb_row = sb("wb_row", [P, ED])
        bo_row = sb("bo_row", [P, D])
        a_col = sb("a_col", [P, 2])
        a_wide = sb("a_wide", [P, 2, P])
        v_src = sb("v_src", [P, D])
        v_dst = sb("v_dst", [P, D])

        sentinel = sb("sentinel", [1, 96], i32)
        src_tab = sb("src_tab", [P, TILES + 2 * G], i32)
        dst_raw = sb("dst_raw", [P, TILES + 2], i32)
        dst_f = sb("dst_f", [P, TILES + 2])
        dst_tab = sb("dst_tab", [P, TILES + 2 * G], i32)
        dst_cl = sb("dst_cl", [P, TILES])
        same_prev = sb("same_prev", [P, TILES])
        same_next = sb("same_next", [P, TILES])
        first = sb("first", [P, TILES])
        first_last = sb("first_last", [P, TILES])
        at_last_f = sb("at_last_f", [P, TILES])
        at_last2_f = sb("at_last2_f", [P, TILES])
        at_last = sb("at_last", [P, TILES + 2 * G], i32)
        at_last2 = sb("at_last2", [P, TILES + 2 * G], i32)
        carry_idx_f = sb("carry_idx_f", [P, 4])
        carry_idx = sb("carry_idx", [P, 2], i32)
        pen_local = sb("pen_local", [P, H, TILES])
        pen_first = sb("pen_first", [P, TILES])
        pen_pad = sb("pen_pad", [P, TILES])

        edge_in = sb("edge_in", [P, TILES * ED])
        edge_mul = sb("edge_mul", [P, G * ED])
        edge_bias = sb("edge_bias", [P, 4, 2, G])
        idx_slot = sb("idx_slot", [P, 4, 2 * G], i32)
        xs = sb("xs", [P, 4, GW])
        xd = sb("xd", [P, 4, GW])
        xsT = sb("xsT", [P, 2, GW])
        xdT = sb("xdT", [P, 2, GW])
        qT = sb("qT", [P, GW])
        prodT = sb("prodT", [P, 2, GW])
        node_in = sb("node_in", [P, 2, BW])
        node_x1 = sb("node_x1", [P, 2, BW])
        node_out = sb("node_out", [P, 2, BW])
        nst = sb("nst", [P, ROWS, 6])
        nmv = sb("nmv", [P, 2, ROWS, 2])
        nstd = sb("nstd", [P, 2, 2, ROWS])
        nsc = sb("nsc", [P, 2, 2, 2, ROWS])
        eps_cols = sb("eps_cols", [P, 2])

        score = sb("score", [P, H, TILES])
        run_max = sb("run_max", [P, H, TILES])
        tmp = sb("tmp", [P, H, TILES])
        weight = sb("weight", [P, H, TILES])
        decay = sb("decay", [P, H, TILES])
        run_sum = sb("run_sum", [P, H, TILES])
        share = sb("share", [P, TILES + G, H])
        ends = sb("ends", [P, 2, H])
        factor_row = sb("factor_row", [H, P])
        carry_row = sb("carry_row", [H, 2, P + 1])
        carry_in = sb("carry_in", [P, H])

        share_slot = sb("share_slot", [P, 2, G * H])
        shareT = sb("shareT", [G * H, 2, P])
        y = sb("y", [P, 2, GW])
        res = sb("res", [P, 4, GW])
        dots = sb("dots", [P, GW])
        yst = sb("yst", [P, G, 6])
        ymv = sb("ymv", [P, 2, G, 2])
        ystd = sb("ystd", [P, 2, G])
        ysc = sb("ysc", [P, 2, 2, G])

        s_src = sb("s_src", [P, TILES])
        s_dst = sb("s_dst", [P, TILES])
        logit = sb("logit", [P, TILES])
        logit2 = sb("logit2", [P, TILES])
        att = sb("att", [P, TILES])
        max_p = sb("max_p", [P, 1])
        max_all = sb("max_all", [1, 1])
        neg_max = sb("neg_max", [P, 1])
        exp_sum = sb("exp_sum", [P, 1])
        inv_sum = sb("inv_sum", [P, 1])
        vT, hT, xa, agg, aggT = (edge_in[:, k * 2 * GW:(k + 1) * 2 * GW].rearrange("p (u w) -> p u w", u=2)
                                 for k in range(5))
        part = sb("part", [P, D])
        diag = sb("diag", [P, P])
        chunkrow = sb("chunkrow", [P, P])
        carryT = sb("carryT", [P, P + 1])
        total = sb("total", [P, D])
        totalT = sb("totalT", [P, D])
        x1c = sb("x1c", [P, D])

        consts_in = sem("consts_in")
        pad_in = sem("pad_in")
        edges_in = sem("edges_in")
        src_in = sem("src_in")
        attr_in = sem("attr_in")
        zeroed = sem("zeroed")
        built = sem("built")
        prep, prep_chain, last_chain = sem("prep"), sem("prep_chain"), sem("last_chain")
        w1T_done, w1T_sb = sem("w1T_done"), sem("w1T_sb")
        v_done = sem("v_done")
        held_pool, held_dve = sem("held_pool"), sem("held_dve")
        idx_ready = sem("idx_ready")
        got_src, got_dst = sems("got_src", 4), sems("got_dst", 4)
        xT_done, xT_sb = sem("xT_done"), sem("xT_sb")
        qk_done, q_sb = sem("qk_done"), sem("q_sb")
        prod_done, s_done, score_done = sem("prod_done"), sem("s_done"), sem("score_done")
        xd_stored = sems("xd_stored", 4)
        bias_chain, node_chain = sem("bias_chain"), sem("node_chain")
        node_loaded = sems("node_loaded", 2)
        node_var, node_std, node_ready, node_applied = (
            sem("node_var"), sem("node_std"), sem("node_ready"), sem("node_applied"))
        x1_stored, out_stored = sems("x1_stored", 2), sems("out_stored", 2)
        soft_chain, ends_ready, ends_T = sem("soft_chain"), sem("ends_ready"), sem("ends_T")
        row_ready, carry_T = sem("row_ready"), sem("carry_T")
        args_ready, exps_done = sem("args_ready"), sem("exps_done")
        share_done = sem("share_done")
        xd_back = sems("xd_back", 4)
        share_cp = sem("share_cp")
        vx_T, vx_Tsb, shT_sb = sem("vx_T"), sem("vx_Tsb"), sem("shT_sb")
        v_mm, v_sb, x_mm, h_done, o_mm = sem("v_mm"), sem("v_sb"), sem("x_mm"), sem("h_done"), sem("o_mm")
        c_var, c_std, c_fin_chain, node_fin_chain = sem("c_var"), sem("c_std"), sem("c_fin_chain"), sem("node_fin_chain")
        e_var, e_std, e_fin_chain = sem("e_var"), sem("e_std"), sem("e_fin_chain")
        c_chain, c_stats, c_applied, sd_chain, sd_done = (
            sem("c_chain"), sem("c_stats"), sem("c_applied"), sem("sd_chain"), sem("sd_done"))
        c_y = sem("c_y")
        c_scat, x1d_stored = sems("c_scat", 4), sems("x1d_stored", 4)
        d_idx, d_got, d_chain, d_done, xs_stored = sem("d_idx"), sems("d_got", 4), sem("d_chain"), sem("d_done"), sems("xs_stored", 4)
        att_chain, max_col, max_T, max_one, max_b = (
            sem("att_chain"), sem("max_col"), sem("max_T"), sem("max_one"), sem("max_b"))
        neg_ready, exp_done, sum_b, att_ready = sem("neg_ready"), sem("exp_done"), sem("sum_b"), sem("att_ready")
        xs_back, x1d_back = sems("xs_back", 4), sems("x1d_back", 4)
        xa_done, r_chain, r_done = sem("xa_done"), sem("r_chain"), sem("r_done")
        e_T, e_Tsb, e_mm, e_chain, e_stats, e_applied = (
            sem("e_T"), sem("e_Tsb"), sem("e_mm"), sem("e_chain"), sem("e_stats"), sem("e_applied"))
        e_y = sem("e_y")
        e_scat = sems("e_scat", 4)
        f_dve, f_pe, f_act, f_got, f_scat = sem("f_dve"), sem("f_pe"), sem("f_act"), sem("f_got"), sem("f_scat")

        block = ctx.enter_context(nc.Block())

        def wait(eng, s, value):
            if not isinstance(value, int) or value > 0:
                eng.wait_ge(s, value)

        def hold(eng, s, value):
            wait(eng, s, value)
            if not isinstance(value, int):
                eng.sem_inc(held_pool if eng is nc.gpsimd else held_dve, 1)

        def pipeline(eng, body, tail=0):
            for g in range(PEEL):
                body(Step(g))
            with eng.Fori(0, LOOPS, 1) as i:
                for off in range(PEEL, PEEL + UNROLL):
                    body(Step(off, i))
            for g in range(GROUPS, GROUPS + tail):
                body(Step(g))

        class Chain:

            def __init__(self, eng, s, per_step, step=None):
                self.eng, self.sem, self.per, self.k = eng, s, per_step, 0
                self.base = 0 if step is None else step.g * per_step

            def link(self, ins):
                self.k += 1
                assert self.per is None or self.k <= self.per
                ins.then_inc(self.sem, 1)
                hold(self.eng, self.sem, self.base + self.k)

        T = lambda a, u, t: a[:, u, t * D:(t + 1) * D]

        def all_done(eng, sems, each):
            for k, s in enumerate(sems):
                eng.wait_ge(s, 16 * each * ((GROUPS - 1 - k) // len(sems) + 1))

        @block.sync
        def _(sp):
            sp.wait_ge(zeroed, 1)
            sp.dma_start(dst_pad[0:1].rearrange("(a b) -> a b", a=1), sentinel[0:1, 0:1]).then_inc(pad_in, 16)
            sp.dma_start(dst_pad[NE + 1:EP + 2].rearrange("(a b) -> a b", a=1),
                         sentinel[0:1, 1:EP + 2 - NE]).then_inc(pad_in, 16)
            sp.dma_start(dst_pad[1:NE + 1].rearrange("(a b) -> a b", a=8),
                         dst.rearrange("(a b) -> a b", a=8)).then_inc(pad_in, 16)
            sp.wait_ge(zeroed, 2)
            head = 112
            main = src[0:head * TILES].rearrange("(p t) -> p t", p=head)
            sp.dma_start(src_tab[0:head, 0:TILES], main).then_inc(src_in, 16)
            sp.dma_start(src_tab[head:P - 1, 0:TILES],
                         src[head * TILES:(P - 1) * TILES].rearrange("(p t) -> p t", t=TILES)).then_inc(src_in, 16)
            sp.dma_start(src_tab[P - 1:P, 0:LASTROW],
                         src[(P - 1) * TILES:NE].rearrange("(p t) -> p t", p=1)).then_inc(src_in, 16)
            sp.wait_ge(pad_in, 48)
            sp.dma_start(dst_raw[:, :], bass.AP(dst_pad, 0, [[TILES, P], [1, TILES + 2]])).then_inc(edges_in, 16)
            for tile, w in ((wq, Wq), (wk, Wk), (wv, Wv), (wo, Wo), (w1, W1)):
                sp.dma_start(tile[:, :], w).then_inc(consts_in, 16)
            for c, b in enumerate((bq, bk, bv)):
                sp.dma_start(bcol[:, c:c + 1], b.rearrange("(p a) -> p a", a=1)).then_inc(consts_in, 16)
            sp.dma_start(bb_col[:, :], bb.rearrange("(p a) -> p a", a=1).to_broadcast([P, 1])).then_inc(consts_in, 16)
            sp.dma_start(wb_row[:, :], Wb.rearrange("e a -> a e").to_broadcast([P, ED])).then_inc(consts_in, 16)
            sp.dma_start(bo_row[:, :], bo.rearrange("(a d) -> a d", a=1).to_broadcast([P, D])).then_inc(consts_in, 16)
            for c in range(2):
                sp.dma_start(a_col[:, c:c + 1], a1[c * D:(c + 1) * D, :]).then_inc(consts_in, 16)
            ev = edge_attr[0:head * TILES, :].rearrange("(p t) e -> p (t e)", p=head)
            sp.dma_start(edge_in[0:head, :], ev).then_inc(attr_in, 16)
            sp.dma_start(edge_in[head:P - 1, :], edge_attr[head * TILES:(P - 1) * TILES, :]
                         .rearrange("(p t) e -> p (t e)", t=TILES)).then_inc(attr_in, 16)
            sp.dma_start(edge_in[P - 1:P, 0:LASTROW * ED], edge_attr[(P - 1) * TILES:NE, :]
                         .rearrange("(p t) e -> p (t e)", p=1)).then_inc(attr_in, 16)

            def stage2(s):
                if s.runs(GROUPS):
                    wait(sp, node_applied, s.g - 1)
                    sp.dma_start(node_in[0:chunk_parts(s), s.u, :], node_chunk(x, s)).then_inc(node_loaded[s.u], 16)
                b = s.back(1)
                if b.runs(GROUPS):
                    wait(sp, got_dst[b.w], b.uses(4) * 16 * G)
                    sp.dma_start(edge_view(xd_rows)[:, bass.ds(b.g * GW, GW)], xd[:, b.w, :]).then_inc(xd_stored[b.w], 16)
                b = s.back(2)
                if b.runs(GROUPS):
                    n = chunk_parts(b)
                    wait(sp, node_applied, b.g + 1)
                    sp.dma_start(node_chunk(x1_table, b), node_x1[0:n, b.u, :]).then_inc(x1_stored[b.u], 16)
                    sp.dma_start(node_chunk(out, b), node_out[0:n, b.u, :]).then_inc(out_stored[b.u], 16)
            pipeline(sp, stage2, 2)
            all_done(sp, xd_stored, 1)

            def stage4(s):
                if s.runs(GROUPS):
                    wait(sp, c_y, s.g - 3)
                    sp.dma_start(xd[:, s.w, :], edge_view(xd_rows)[:, bass.ds(s.g * GW, GW)]).then_inc(xd_back[s.w], 16)
                b = s.back(5)
                if b.runs(GROUPS):
                    wait(sp, c_applied, b.g + 1)
                    sp.dma_start(edge_view(x1d_rows)[:, bass.ds(b.g * GW, GW)], res[:, b.w, :]).then_inc(x1d_stored[b.w], 16)
            sp.wait_ge(score_done, GROUPS)
            pipeline(sp, stage4, 5)

            def stage5(s):
                wait(sp, d_got[s.w], s.uses(4) * 16 * G)
                sp.dma_start(edge_view(xs_rows)[:, bass.ds(s.g * GW, GW)], xs[:, s.w, :]).then_inc(xs_stored[s.w], 16)
            pipeline(sp, stage5)
            all_done(sp, xs_stored, 1)
            all_done(sp, x1d_stored, 1)
            sp.wait_ge(d_done, GROUPS)

            def stage7(s):
                wait(sp, xa_done, s.g - 3)
                sp.dma_start(xs[:, s.w, :], edge_view(xs_rows)[:, bass.ds(s.g * GW, GW)]).then_inc(xs_back[s.w], 16)
                wait(sp, e_y, s.g - 3)
                sp.dma_start(xd[:, s.w, :], edge_view(x1d_rows)[:, bass.ds(s.g * GW, GW)]).then_inc(x1d_back[s.w], 16)
            pipeline(sp, stage7)
            all_done(sp, out_stored, 1)
            all_done(sp, e_scat, G)
            sp.wait_ge(f_scat, 16)

        @block.gpsimd
        def _(pool):
            pool.memset(sentinel[:, :], N).then_inc(built, 1)
            pool.wait_ge(built, 1)
            pool.memset(sentinel[:, 0:1], -1).then_inc(zeroed, 1)
            pool.memset(src_tab[:, :], 0)
            pool.memset(edge_in[:, LASTROW * ED:TILES * ED], 0.0).then_inc(zeroed, 1)
            pool.memset(ident[:, :], 0.0)
            pool.memset(expand[:, :, :], 0.0)
            pool.memset(head_sel[:, :], 1.0).then_inc(built, 1)
            pool.wait_ge(built, 2)
            pool.affine_select(out=ident[:, :], in_=ident[:, :], compare_op=ALU.not_equal, fill=1.0,
                               base=0, pattern=[[-1, P]], channel_multiplier=1)
            ex = expand[:, :, :].rearrange("q t (h c) -> q t h c", h=H)
            pool.affine_select(out=ex, in_=ex, compare_op=ALU.not_equal, fill=1.0,
                               base=0, pattern=[[-H, G], [-1, H], [0, HD]], channel_multiplier=1)
            pool.affine_select(out=head_sel[:, :], in_=head_sel[:, :], compare_op=ALU.is_ge, fill=0.0,
                               base=0, pattern=[[-HD, H]], channel_multiplier=1).then_inc(built, 1)
            pool.wait_ge(built, 3)
            pool.affine_select(out=head_sel[:, :], in_=head_sel[:, :], compare_op=ALU.is_ge, fill=0.0,
                               base=HD - 1, pattern=[[HD, H]], channel_multiplier=-1).then_inc(built, 1)

            def rows(tile, u, t):
                return tile[:, u, t * D:(t + 1) * D]

            def gather(tile, table, idx, u, t, done):
                pool.indirect_dma_start(out=rows(tile, u, t), out_offset=None, in_=table,
                                        in_offset=bass.IndirectOffsetOnAxis(ap=idx, axis=0))\
                    .then_inc(done, 16)

            def scatter(table, tile, idx, u, t, done):
                pool.indirect_dma_start(out=table, out_offset=bass.IndirectOffsetOnAxis(ap=idx, axis=0),
                                        in_=rows(tile, u, t), in_offset=None,
                                        bounds_check=N - 1, oob_is_err=False).then_inc(done, 16)

            def stage2(s):
                hold(pool, idx_ready, s.g + 1)
                hold(pool, xT_done, s.g - 3)
                for t in range(G):
                    gather(xs, x, idx_slot[:, s.w, t:t + 1], s.w, t, got_src[s.w])
                hold(pool, xd_stored[s.w], s.back(4).uses(4) * 16)
                for t in range(G):
                    gather(xd, x, idx_slot[:, s.w, G + t:G + t + 1], s.w, t, got_dst[s.w])
            pipeline(pool, stage2)
            all_done(pool, x1_stored, 1)

            def stage4(s):
                hold(pool, c_applied, s.g + 1)
                for t in range(G):
                    scatter(x1_table, res, idx_slot[:, s.w, t:t + 1], s.w, t, c_scat[s.w])
            pipeline(pool, stage4)
            all_done(pool, c_scat, G)

            def stage5(s):
                hold(pool, d_idx, s.g + 1)
                hold(pool, d_done, s.g - 3)
                hold(pool, xs_stored[s.w], s.back(4).uses(4) * 16)
                for t in range(G):
                    gather(xs, x1_table, idx_slot[:, s.w, t:t + 1], s.w, t, d_got[s.w])
            pipeline(pool, stage5)
            gather_c = pool.indirect_dma_start(out=x1c[:, :], out_offset=None, in_=x1_table,
                                               in_offset=bass.IndirectOffsetOnAxis(ap=carry_idx[:, 0:1], axis=0))
            gather_c.then_inc(f_got, 16)
            all_done(pool, out_stored, 1)

            def stage7(s):
                hold(pool, e_applied, s.g + 1)
                for t in range(G):
                    scatter(out, res, idx_slot[:, s.w, t:t + 1], s.w, t, e_scat[s.w])
            pipeline(pool, stage7)
            pool.wait_ge(f_act, 3)
            pool.indirect_dma_start(out=out, out_offset=bass.IndirectOffsetOnAxis(ap=carry_idx[:, 1:2], axis=0),
                                    in_=total[:, :], in_offset=None,
                                    bounds_check=N - 1, oob_is_err=False).then_inc(f_scat, 16)

        @block.tensor
        def _(pe):
            mm, tr = nc.tensor.matmul, nc.tensor.transpose
            pe.wait_ge(consts_in, 16 * 13)
            pe.wait_ge(built, 4)
            tr(bank[0][:, 0:P], w1[:, :], ident[:, :]).then_inc(w1T_done, 1)
            pe.wait_ge(w1T_sb, 1)
            pe.wait_ge(prep, 1)
            for c in range(2):
                last = mm(bank[1][:, c * D:(c + 1) * D], a_wide[:, c, :], w1T[:, :], start=True, stop=True)
            last.then_inc(v_done, 1)

            def stage2(s):
                if s.runs(GROUPS):
                    wait(pe, got_src[s.w], s.uses(4) * 16 * G)
                    wait(pe, got_dst[s.w], s.uses(4) * 16 * G)
                    wait(pe, xT_sb, s.g * 2)
                    for t in range(G):
                        tr(bank[2][:, t * P:(t + 1) * P], T(xs, s.w, t), ident[:, :])
                    for t in range(G):
                        last = tr(bank[3][:, t * P:(t + 1) * P], T(xd, s.w, t), ident[:, :])
                    last.then_inc(xT_done, 1)
                b = s.back(1)
                if b.runs(GROUPS):
                    wait(pe, xT_sb, b.g * 2 + 2)
                    wait(pe, q_sb, b.g)
                    wait(pe, prod_done, b.g)
                    mm(bank[4][:, :], wq[:, :], xsT[:, b.u, :], start=True, stop=True)
                    mm(bank[5][:, :], wk[:, :], xdT[:, b.u, :], start=True, stop=True).then_inc(qk_done, 1)
                b = s.back(2)
                if b.runs(GROUPS):
                    wait(pe, prod_done, b.g + 1)
                    wait(pe, score_done, b.g - 1)
                    for t in range(G):
                        last = mm(bank[6 + b.u][:, t * H:(t + 1) * H], prodT[:, b.u, t * P:(t + 1) * P],
                                  head_sel[:, :], start=True, stop=True)
                    last.then_inc(s_done, 1)
            pe.wait_ge(prep, 2)
            pipeline(pe, stage2, 2)

            for k in range(2):
                pe.wait_ge(ends_ready, k + 1)
                tr(bank[0][0:H, 0:P], ends[:, 0, :], ident[:, :])
                tr(bank[0][0:H, P:2 * P], ends[:, 1, :], ident[:, :]).then_inc(ends_T, 1)
                pe.wait_ge(row_ready, k + 1)
                tr(bank[1][:, 0:H], carry_row[:, k, 0:P], ident[0:H, 0:H]).then_inc(carry_T, 1)

            def stage4(s):
                if s.runs(GROUPS):
                    wait(pe, xd_back[s.w], s.uses(4) * 16)
                    wait(pe, vx_Tsb, s.g)
                    for t in range(G):
                        tr(bank[2][:, t * P:(t + 1) * P], T(xd, s.w, t), ident[:, :])
                    wait(pe, shT_sb, s.g)
                    wait(pe, share_cp, s.g + 1)
                    tr(bank[3][0:G * H, 0:P], share_slot[:, s.u, :], ident[:, :]).then_inc(vx_T, 1)
                b = s.back(1)
                if b.runs(GROUPS):
                    wait(pe, vx_Tsb, b.g + 1)
                    wait(pe, v_sb, b.g - 1)
                    mm(bank[4 + b.u][:, :], wv[:, :], xdT[:, b.u, :], start=True, stop=True).then_inc(v_mm, 1)
                    wait(pe, shT_sb, b.g + 1)
                    wait(pe, h_done, b.g - 1)
                    for t in range(G):
                        last = mm(bank[6 + b.u][:, t * P:(t + 1) * P], expand[:, t, :], shareT[:, b.u, :],
                                  start=True, stop=True)
                    last.then_inc(x_mm, 1)
                b = s.back(2)
                if b.runs(GROUPS):
                    wait(pe, h_done, b.g + 1)
                    wait(pe, c_y, b.g - 1)
                    for t in range(G):
                        last = mm(bank[b.u][:, t * D:(t + 1) * D], T(hT, b.u, t), wo[:, :], start=True, stop=True)
                    last.then_inc(o_mm, 1)
            pe.wait_ge(share_done, 1)
            pipeline(pe, stage4, 2)

            pe.wait_ge(max_col, 1)
            tr(bank[2][0:1, 0:P], max_p[:, :], ident[:, :]).then_inc(max_T, 1)
            pe.wait_ge(max_one, 1)
            mm(bank[3][:, 0:1], ones[0:1, :], max_all[:, :], start=True, stop=True).then_inc(max_b, 1)
            pe.wait_ge(exp_done, 1)
            mm(bank[4][:, 0:1], ones[:, :], exp_sum[:, :], start=True, stop=True)
            mm(bank[5][:, 0:P], ones[:, :], diag[:, :], start=True, stop=True).then_inc(sum_b, 1)
            pe.wait_ge(att_ready, 1)

            def stage7(s):
                b = s.back(1)
                if b.runs(GROUPS):
                    wait(pe, e_Tsb, b.g + 1)
                    wait(pe, e_y, b.g - 1)
                    for t in range(G):
                        last = mm(bank[b.u][:, t * D:(t + 1) * D], T(aggT, b.u, t), w1[:, :], start=True, stop=True)
                    last.then_inc(e_mm, 1)
                if s.runs(GROUPS):
                    wait(pe, r_done, s.g + 1)
                    wait(pe, e_Tsb, s.g - 1)
                    for t in range(G):
                        last = tr(bank[2 + s.u][:, t * P:(t + 1) * P], T(agg, s.u, t), ident[:, :])
                    last.then_inc(e_T, 1)
            pipeline(pe, stage7, 1)
            tr(bank[4][:, 0:P], T(agg, (GROUPS - 1) % 2, G - 1), ident[:, :]).then_inc(f_pe, 1)
            pe.wait_ge(f_dve, 1)
            tr(bank[5][:, 0:P], carryT[:, 0:P], ident[:, :]).then_inc(f_pe, 1)
            pe.wait_ge(f_dve, 2)
            tr(bank[6][:, 0:P], total[:, :], ident[:, :]).then_inc(f_pe, 1)
            pe.wait_ge(f_act, 1)
            mm(bank[7][:, 0:D], totalT[:, :], w1[:, :], start=True, stop=True).then_inc(f_pe, 1)

        @block.scalar
        def _(act):
            fn = nc.scalar.activation
            act.wait_ge(w1T_done, 1)
            fn(w1T[:, :], bank[0][:, 0:P], ACT.Copy).then_inc(w1T_sb, 1)

            def stage2(s):
                b = s.back(1)
                if b.runs(GROUPS):
                    n = chunk_parts(b)
                    wait(act, node_var, b.g + 1)
                    wait(act, node_ready, b.g - 1)
                    var = nmv[0:n, b.u, :, 1]
                    fn(nstd[0:n, b.u, 0, :], var, ACT.Sqrt, bias=eps_cols[0:n, 0:1])
                    fn(nstd[0:n, b.u, 1, :], var, ACT.Sqrt, bias=eps_cols[0:n, 1:2], scale=1.0 + EPS)\
                        .then_inc(node_std, 1)
                if s.runs(GROUPS):
                    wait(act, xT_done, s.g + 1)
                    wait(act, qk_done, s.g - 1)
                    fn(xsT[:, s.u, :], bank[2][:, :], ACT.Copy).then_inc(xT_sb, 1)
                    fn(xdT[:, s.u, :], bank[3][:, :], ACT.Copy).then_inc(xT_sb, 1)
                if b.runs(GROUPS):
                    wait(act, qk_done, b.g + 1)
                    wait(act, prod_done, b.g)
                    fn(qT[:, :], bank[4][:, :], ACT.Identity, bias=bcol[:, 0:1]).then_inc(q_sb, 1)
                    wait(act, node_ready, b.g + 1)
                    wait(act, x1_stored[b.u], b.back(2).uses(2) * 16)
                    wait(act, out_stored[b.u], b.back(2).uses(2) * 16)
                    for r in range(ROWS):
                        cols = slice(r * D, (r + 1) * D)
                        for k, to in enumerate((node_x1, node_out)):
                            last = fn(to[0:n, b.u, cols], node_in[0:n, b.u, cols], ACT.Identity,
                                      bias=nsc[0:n, b.u, 1, k, r:r + 1], scale=nsc[0:n, b.u, 0, k, r:r + 1])
                    last.then_inc(node_applied, 1)
            act.wait_ge(consts_in, 16 * 13)
            pipeline(act, stage2, 1)

            for k in range(3):
                act.wait_ge(args_ready, k + 1)
                e = (weight, decay, tmp)[k]
                fn(e[:, :, :], e[:, :, :], ACT.Exp).then_inc(exps_done, 1)
            act.wait_ge(share_done, 1)

            def apply(b, stats, done, at, first_free):
                wait(act, stats, b.g + 1)
                first_free()
                fn(idx_slot[:, b.w, 0:G], at[:, bass.ds(b.g * G, G)], ACT.Copy)
                for t in range(G):
                    last = fn(T(res, b.w, t), T(y, b.u, t), ACT.Identity,
                              bias=ysc[:, b.u, 1, t:t + 1], scale=ysc[:, b.u, 0, t:t + 1])
                last.then_inc(done, 1)

            def deviation(b, var_ready, std_ready, stats):
                wait(act, var_ready, b.g + 1)
                wait(act, stats, b.g - 1)
                fn(ystd[:, b.u, :], ymv[:, b.u, :, 1], ACT.Sqrt, bias=eps_cols[:, 0:1]).then_inc(std_ready, 1)

            def copy_shares(off, step):
                u = (step.off + off) % 2
                fn(share_slot[:, u, :].rearrange("p (t h) -> p t h", t=G), share[:, bass.ds((step.g + off) * G, G), :],
                   ACT.Copy).then_inc(share_cp, 1)
            copy_shares(0, Step(0))

            def stage4(s):
                b = s.back(3)
                if b.runs(GROUPS):
                    deviation(b, c_var, c_std, c_stats)
                if s.runs(GROUPS):
                    wait(act, vx_T, s.g + 1)
                    wait(act, v_mm, s.g - 1)
                    fn(xdT[:, s.u, :], bank[2][:, :], ACT.Copy).then_inc(vx_Tsb, 1)
                    copy_shares(1, s)
                    wait(act, x_mm, s.g - 1)
                    fn(shareT[:, s.u, :], bank[3][0:G * H, 0:P], ACT.Copy).then_inc(shT_sb, 1)
                a = s.back(1)
                if a.runs(GROUPS):
                    wait(act, v_mm, a.g + 1)
                    wait(act, h_done, a.g - 1)
                    fn(vT[:, a.u, :], bank[4 + a.u][:, :], ACT.Identity, bias=bcol[:, 2:3]).then_inc(v_sb, 1)
                if b.runs(GROUPS):
                    def free():
                        wait(act, sd_done, b.g - 3)
                        wait(act, x1d_stored[b.w], b.back(4).uses(4) * 16)
                        wait(act, c_scat[b.w], b.back(4).uses(4) * 16 * G)
                    apply(b, c_stats, c_applied, at_last, free)
            pipeline(act, stage4, 3)

            act.wait_ge(neg_ready, 1)
            fn(att[:, :], logit[:, :], ACT.Exp, bias=neg_max[:, :], accum_out=exp_sum[:, :]).then_inc(exp_done, 1)
            act.wait_ge(att_ready, 1)
            all_done(act, x1d_stored, 1)
            all_done(act, c_scat, G)

            def stage7(s):
                b = s.back(3)
                if b.runs(GROUPS):
                    deviation(b, e_var, e_std, e_stats)
                if s.runs(GROUPS):
                    wait(act, xs_back[s.w], s.uses(4) * 16)
                    wait(act, r_done, s.g - 1)
                    for t in range(G):
                        last = fn(T(xa, s.u, t), T(xs, s.w, t), ACT.Copy, scale=att[:, bass.ds(s.g * G + t, 1)])
                    last.then_inc(xa_done, 1)
                a = s.back(1)
                if a.runs(GROUPS):
                    wait(act, e_T, a.g + 1)
                    wait(act, e_mm, a.g - 1)
                    fn(aggT[:, a.u, :], bank[2 + a.u][:, :], ACT.Copy).then_inc(e_Tsb, 1)
                if b.runs(GROUPS):
                    apply(b, e_stats, e_applied, at_last2,
                          lambda: wait(act, e_scat[b.w], b.back(4).uses(4) * 16 * G))
            pipeline(act, stage7, 3)
            act.wait_ge(f_pe, 3)
            fn(totalT[:, :], bank[6][:, 0:P], ACT.Copy).then_inc(f_act, 1)
            act.wait_ge(f_dve, 3)
            fn(ystd[:, 0, 0:1], ymv[:, 0, 0, 1:2], ACT.Sqrt, bias=eps_cols[:, 0:1]).then_inc(f_act, 1)
            act.wait_ge(f_dve, 4)
            fn(total[:, :], y[:, 0, 0:D], ACT.Identity, bias=ysc[:, 0, 1, 0:1], scale=ysc[:, 0, 0, 0:1])\
                .then_inc(f_act, 1)

        @block.vector
        def _(dve):
            v = nc.vector
            chain = Chain(dve, prep_chain, None)
            v.memset(ones[:, :], 1.0)
            v.memset(eps_cols[:, 0:1], EPS)
            v.memset(eps_cols[:, 1:2], EPS * EPS)
            v.memset(dst_tab[:, TILES:], 0)
            v.memset(part[:, :], 0.0)
            v.memset(carryT[:, 0:1], 0.0)
            v.memset(carry_row[:, 0, 0:1], -BIG)
            v.memset(decay[:, :, 0:1], -BIG)
            v.memset(share[:, TILES:, :], 0.0)
            v.memset(carry_row[:, 1, 0:1], 0.0)
            dve.wait_ge(consts_in, 16 * 13)
            for c in range(2):
                last = v.tensor_copy(a_wide[:, c, :], a_col[:, c:c + 1].to_broadcast([P, P]))
            last.then_inc(prep, 1)
            dve.wait_ge(edges_in, 16)
            chain.link(v.tensor_copy(dst_f[:, :], dst_raw[:, :]))
            cur, prv, nxt = dst_f[:, 1:TILES + 1], dst_f[:, 0:TILES], dst_f[:, 2:TILES + 2]
            v.tensor_scalar(dst_cl[:, :], cur, float(N - 1), None, ALU.min)
            v.tensor_tensor(same_prev[:, :], cur, prv, ALU.is_equal)
            v.tensor_tensor(same_next[:, :], cur, nxt, ALU.is_equal)
            v.tensor_scalar(pen_pad[:, :], cur, float(N), -BIG, ALU.is_ge, ALU.mult)
            chain.link(v.tensor_scalar(first[:, :], cur, dst_f[:, 0:1], None, ALU.is_equal))
            v.tensor_copy(dst_tab[:, 0:TILES], dst_cl[:, :])
            v.memset(same_prev[:, 0:1], 0.0)
            v.scalar_tensor_tensor(at_last_f[:, :], same_next[:, :], SKIP, cur, ALU.mult, ALU.add)
            v.tensor_scalar(pen_first[:, :], first[:, :], 1.0, BIG, ALU.subtract, ALU.mult)
            v.tensor_tensor(first_last[:, :], first[:, :], same_next[:, :], ALU.mult)
            v.tensor_scalar(carry_idx_f[:, 0:1], dst_f[:, 0:1], 0.0, float(N - 1), ALU.max, ALU.min)
            v.tensor_tensor(carry_idx_f[:, 2:3], dst_f[:, TILES + 1:TILES + 2], dst_f[:, 0:1], ALU.is_equal)
            dve.wait_ge(built, 4)
            chain.link(v.tensor_scalar(diag[:, :], ident[:, :], first[:, TILES - 1:TILES], None, ALU.mult))
            v.tensor_tensor(first_last[:, :], first[:, :], first_last[:, :], ALU.subtract)
            v.tensor_copy(at_last[:, 0:TILES], at_last_f[:, :])
            v.scalar_tensor_tensor(at_last2_f[:, :], first[:, :], SKIP, at_last_f[:, :], ALU.mult, ALU.add)
            v.tensor_copy(carry_idx[:, 0:1], carry_idx_f[:, 0:1])
            chain.link(v.tensor_tensor(carry_idx_f[:, 3:4], carry_idx_f[:, 2:3], first[:, 0:1], ALU.subtract))
            v.tensor_copy(at_last2[:, 0:TILES], at_last2_f[:, :])
            chain.link(v.tensor_scalar(carry_idx_f[:, 2:3], carry_idx_f[:, 3:4], 1.0, SKIP, ALU.add, ALU.mult))
            chain.link(v.tensor_tensor(carry_idx_f[:, 3:4], carry_idx_f[:, 2:3], dst_f[:, 0:1], ALU.add))
            v.tensor_copy(carry_idx[:, 1:2], carry_idx_f[:, 3:4])
            v.tensor_copy(ends[:, 1, :], pen_first[:, TILES - 1:TILES].to_broadcast([P, H]))
            v.tensor_scalar(pen_local[:, :, :], same_prev[:, :].unsqueeze(1).to_broadcast([P, H, TILES]),
                            1.0, BIG, ALU.subtract, ALU.mult)
            dve.wait_ge(src_in, 48)
            dve.wait_ge(v_done, 1)
            v.tensor_copy(v_src[:, :], bank[1][:, 0:D])
            v.tensor_copy(v_dst[:, :], bank[1][:, D:2 * D]).then_inc(prep, 1)

            def fetch_indices(s, both, ready):
                at = bass.ds((s.g + 2) * G, G)
                w = (s.w + 2) % 4
                last = v.tensor_copy(idx_slot[:, w, 0:G], src_tab[:, at])
                if both:
                    last = v.tensor_copy(idx_slot[:, w, G:2 * G], dst_tab[:, at])
                last.then_inc(ready, 1)

            def stage2(s):
                b = s.back(1)
                if b.runs(GROUPS):
                    n = chunk_parts(b)
                    c = Chain(dve, node_fin_chain, 1, b)
                    wait(dve, node_std, b.g + 1)
                    wait(dve, node_applied, b.g - 1)
                    c.link(v.reciprocal(nsc[0:n, b.u, 0, :, :], nstd[0:n, b.u, :, :]))
                    v.scalar_tensor_tensor(nsc[0:n, b.u, 1, :, :],
                                           nmv[0:n, b.u, :, 0].unsqueeze(1).to_broadcast([n, 2, ROWS]), -1.0,
                                           nsc[0:n, b.u, 0, :, :], ALU.mult, ALU.mult).then_inc(node_ready, 1)
                    wait(dve, q_sb, b.g + 1)
                    wait(dve, s_done, b.g - 1)
                    v.scalar_tensor_tensor(prodT[:, b.u, :], bank[5][:, :], bcol[:, 1:2], qT[:, :],
                                           ALU.add, ALU.mult).then_inc(prod_done, 1)
                if s.runs(GROUPS):
                    ahead = s.back(2)
                    wait(dve, got_src[ahead.w], ahead.uses(4) * 16 * G)
                    wait(dve, got_dst[ahead.w], ahead.uses(4) * 16 * G)
                    fetch_indices(s, True, idx_ready)
                    c = Chain(dve, bias_chain, 3, s)
                    cols = bass.ds(s.g * G * ED, G * ED)
                    mul = edge_mul[:, :].rearrange("p (t e) -> p t e", t=G)
                    c.link(v.tensor_tensor(mul, edge_in[:, cols].rearrange("p (t e) -> p t e", t=G),
                                           wb_row[:, :].unsqueeze(1).to_broadcast([P, G, ED]), ALU.mult))
                    c.link(v.tensor_reduce(edge_bias[:, s.w, 0, :], mul, AX, ALU.add))
                    c.link(v.tensor_scalar(edge_bias[:, s.w, 1, :], edge_bias[:, s.w, 0, :], bb_col[:, :], None,
                                           ALU.add))
                    n = chunk_parts(s)
                    c = Chain(dve, node_chain, 2, s)
                    yv = node_in[0:n, s.u, :].rearrange("p (r d) -> p r d", r=ROWS)
                    wait(dve, node_loaded[s.u], s.uses(2) * 16)
                    c.link(v.tensor_tensor(yv, yv, bo_row[0:n, :].unsqueeze(1).to_broadcast([n, ROWS, D]), ALU.add))
                    for r in range(ROWS):
                        last = v.bn_stats(nst[0:n, r, :], node_in[0:n, s.u, r * D:(r + 1) * D])
                    c.link(last)
                    for r in range(ROWS):
                        last = v.bn_aggr(nmv[0:n, s.u, r, :], nst[0:n, r, :])
                    last.then_inc(node_var, 1)
                b = s.back(2)
                if b.runs(GROUPS):
                    wait(dve, s_done, b.g + 1)
                    v.scalar_tensor_tensor(score[:, :, bass.ds(b.g * G, G)],
                                           bank[6 + b.u][:, 0:G * H].rearrange("p (t h) -> p h t", t=G),
                                           float(HD) ** -0.5,
                                           edge_bias[:, b.w, 1, :].unsqueeze(1).to_broadcast([P, H, G]),
                                           ALU.mult, ALU.add).then_inc(score_done, 1)
            fetch_indices(Step(-2), True, idx_ready)
            fetch_indices(Step(-1), True, idx_ready)
            dve.wait_ge(attr_in, 48)
            pipeline(dve, stage2, 2)

            flat = lambda a: a[:, :, :].rearrange("p h t -> p (h t)")
            along = lambda a: a.unsqueeze(1).to_broadcast([P, H, TILES])
            over = lambda a: a.unsqueeze(2).to_broadcast([P, H, TILES])
            c = Chain(dve, soft_chain, None)
            dve.wait_ge(score_done, GROUPS)
            c.link(v.tensor_tensor_scan(flat(run_max), flat(pen_local), flat(score), -BIG, ALU.add, ALU.max))
            v.tensor_copy(ends[:, 0, :], run_max[:, :, TILES - 1]).then_inc(ends_ready, 1)
            dve.wait_ge(ends_T, 1)
            c.link(v.tensor_copy(factor_row[:, :], bank[0][0:H, P:2 * P]))
            v.tensor_tensor_scan(carry_row[:, 0, 1:P + 1], factor_row[:, :], bank[0][0:H, 0:P], -BIG,
                                 ALU.add, ALU.max).then_inc(row_ready, 1)
            dve.wait_ge(carry_T, 1)
            c.link(v.tensor_copy(carry_in[:, :], bank[1][:, 0:H]))
            c.link(v.tensor_tensor(tmp[:, :, :], along(pen_first[:, :]), over(carry_in[:, :]), ALU.add))
            c.link(v.tensor_tensor(run_max[:, :, :], run_max[:, :, :], tmp[:, :, :], ALU.max))
            v.tensor_tensor(weight[:, :, :], score[:, :, :], run_max[:, :, :], ALU.subtract).then_inc(args_ready, 1)
            c.link(v.tensor_tensor(decay[:, :, 1:TILES], run_max[:, :, 0:TILES - 1], run_max[:, :, 1:TILES],
                                   ALU.subtract))
            v.tensor_tensor(decay[:, :, 1:TILES], decay[:, :, 1:TILES], pen_local[:, :, 1:TILES], ALU.add)\
                .then_inc(args_ready, 1)
            v.tensor_tensor(tmp[:, :, :], tmp[:, :, :], run_max[:, :, :], ALU.subtract).then_inc(args_ready, 1)
            dve.wait_ge(exps_done, 3)
            c.link(v.tensor_tensor_scan(flat(run_sum), flat(decay), flat(weight), 0.0, ALU.mult, ALU.add))
            v.tensor_copy(ends[:, 1, :], tmp[:, :, TILES - 1])
            v.tensor_copy(ends[:, 0, :], run_sum[:, :, TILES - 1]).then_inc(ends_ready, 1)
            dve.wait_ge(ends_T, 2)
            c.link(v.tensor_copy(factor_row[:, :], bank[0][0:H, P:2 * P]))
            v.tensor_tensor_scan(carry_row[:, 1, 1:P + 1], factor_row[:, :], bank[0][0:H, 0:P], 0.0,
                                 ALU.mult, ALU.add).then_inc(row_ready, 1)
            dve.wait_ge(carry_T, 2)
            c.link(v.tensor_copy(carry_in[:, :], bank[1][:, 0:H]))
            c.link(v.tensor_tensor(tmp[:, :, :], tmp[:, :, :], over(carry_in[:, :]), ALU.mult))
            c.link(v.tensor_tensor(run_sum[:, :, :], run_sum[:, :, :], tmp[:, :, :], ALU.add))
            c.link(v.reciprocal(decay[:, :, :], run_sum[:, :, :]))
            v.tensor_tensor(share[:, 0:TILES, :].rearrange("p t h -> p h t"), run_sum[:, :, :], decay[:, :, :], ALU.mult)\
                .then_inc(share_done, 1)

            def tail(b, o_ready, y_done, chain_sem, var_ready, applied, bias=None):
                c = Chain(dve, chain_sem, 2 if bias else 1, b)
                wait(dve, o_ready, b.g + 1)
                wait(dve, applied, b.g - 1)
                ins = v.tensor_tensor(y[:, b.u, :], xd[:, b.w, :], bank[b.u][:, :], ALU.add)
                ins.then_inc(y_done, 1)
                wait(dve, y_done, b.g + 1)
                if bias:
                    yv = y[:, b.u, :].rearrange("p (t d) -> p t d", t=G)
                    c.link(v.tensor_tensor(yv, yv, bias[:, :].unsqueeze(1).to_broadcast([P, G, D]), ALU.add))
                for t in range(G):
                    last = v.bn_stats(yst[:, t, :], T(y, b.u, t))
                c.link(last)
                for t in range(G):
                    last = v.bn_aggr(ymv[:, b.u, t, :], yst[:, t, :])
                last.then_inc(var_ready, 1)

            def finish(b, chain_sem, std_ready, stats_done, applied):
                c = Chain(dve, chain_sem, 1, b)
                wait(dve, std_ready, b.g + 1)
                wait(dve, applied, b.g - 1)
                c.link(v.reciprocal(ysc[:, b.u, 0, :], ystd[:, b.u, :]))
                v.scalar_tensor_tensor(ysc[:, b.u, 1, :], ymv[:, b.u, :, 0], -1.0, ysc[:, b.u, 0, :],
                                       ALU.mult, ALU.mult).then_inc(stats_done, 1)

            def dot(rows, vector, scores, b, chain_sem, done):
                c = Chain(dve, chain_sem, 1, b)
                wait(dve, done, b.g)
                wide = lambda a: a.rearrange("p (t d) -> p t d", t=G)
                c.link(v.tensor_tensor(wide(dots[:, :]), wide(rows[:, b.w, :]),
                                       vector[:, :].unsqueeze(1).to_broadcast([P, G, D]), ALU.mult))
                v.tensor_reduce(scores[:, bass.ds(b.g * G, G)], wide(dots[:, :]), AX, ALU.add).then_inc(done, 1)

            def stage4(s):
                b = s.back(3)
                if b.runs(GROUPS):
                    finish(b, c_fin_chain, c_std, c_stats, c_applied)
                b = s.back(1)
                if b.runs(GROUPS):
                    wait(dve, v_sb, b.g + 1)
                    wait(dve, x_mm, b.g + 1)
                    wait(dve, o_mm, b.g - 1)
                    v.tensor_tensor(hT[:, b.u, :], vT[:, b.u, :], bank[6 + b.u][:, :], ALU.mult).then_inc(h_done, 1)
                b = s.back(2)
                if b.runs(GROUPS):
                    tail(b, o_mm, c_y, c_chain, c_var, c_applied, bo_row)
                b = s.back(4)
                if b.runs(GROUPS):
                    wait(dve, c_applied, b.g + 1)
                    dot(res, v_dst, s_dst, b, sd_chain, sd_done)
            pipeline(dve, stage4, 4)
            all_done(dve, c_scat, G)
            fetch_indices(Step(-2), False, d_idx)
            fetch_indices(Step(-1), False, d_idx)

            def stage5(s):
                wait(dve, d_got[s.w], s.uses(4) * 16 * G)
                fetch_indices(s, False, d_idx)
                dot(xs, v_src, s_src, s, d_chain, d_done)
            pipeline(dve, stage5)

            v.memset(agg[:, 1, (G - 1) * D:G * D], 0.0)
            c = Chain(dve, att_chain, None)
            dve.wait_ge(d_done, GROUPS)
            c.link(v.tensor_tensor(logit[:, :], s_src[:, :], s_dst[:, :], ALU.add))
            c.link(v.scalar_tensor_tensor(logit2[:, :], logit[:, :], SLOPE, logit[:, :], ALU.mult, ALU.max))
            c.link(v.tensor_tensor(logit[:, :], logit2[:, :], pen_pad[:, :], ALU.add))
            v.tensor_reduce(max_p[:, :], logit[:, :], AX, ALU.max).then_inc(max_col, 1)
            dve.wait_ge(max_T, 1)
            v.tensor_reduce(max_all[:, :], bank[2][0:1, 0:P], AX, ALU.max).then_inc(max_one, 1)
            dve.wait_ge(max_b, 1)
            v.tensor_scalar(neg_max[:, :], bank[3][:, 0:1], -1.0, None, ALU.mult).then_inc(neg_ready, 1)
            dve.wait_ge(sum_b, 1)
            v.tensor_copy(chunkrow[:, :], bank[5][:, 0:P])
            c.link(v.reciprocal(inv_sum[:, :], bank[4][:, 0:1]))
            v.tensor_scalar(att[:, :], att[:, :], inv_sum[:, :], None, ALU.mult).then_inc(att_ready, 1)

            def stage7(s):
                b = s.back(3)
                if b.runs(GROUPS):
                    finish(b, e_fin_chain, e_std, e_stats, e_applied)
                b = s.back(2)
                if b.runs(GROUPS):
                    wait(dve, x1d_back[b.w], b.uses(4) * 16)
                    tail(b, e_mm, e_y, e_chain, e_var, e_applied)
                if s.runs(GROUPS):
                    c = Chain(dve, r_chain, 7, s)
                    wait(dve, xa_done, s.g + 1)
                    wait(dve, e_T, s.g - 1)
                    col = lambda tab, t: tab[:, bass.ds(s.g * G + t, 1)]

                    def own(t):
                        return v.scalar_tensor_tensor(part[:, :], T(agg, s.u, t), col(first_last, t), part[:, :],
                                                      ALU.mult, ALU.add)
                    for t in range(G):
                        prev = T(agg, s.u, t - 1) if t else T(agg, 1 - s.u, G - 1)
                        ins = v.scalar_tensor_tensor(T(agg, s.u, t), prev, col(same_prev, t), T(xa, s.u, t),
                                                     ALU.mult, ALU.add)
                        if t == G - 1:
                            ins.then_inc(r_done, 1)
                            wait(dve, r_done, s.g + 1)
                        else:
                            c.link(ins)
                        if t:
                            c.link(own(t - 1))
                    c.link(own(G - 1))
            pipeline(dve, stage7, 3)

            c = Chain(dve, last_chain, None)
            dve.wait_ge(f_pe, 1)
            v.tensor_tensor_scan(carryT[:, 1:P + 1], chunkrow[:, :], bank[4][:, 0:P], 0.0, ALU.mult, ALU.add)\
                .then_inc(f_dve, 1)
            dve.wait_ge(f_pe, 2)
            v.tensor_tensor(total[:, :], part[:, :], bank[5][:, 0:P], ALU.add).then_inc(f_dve, 1)
            dve.wait_ge(f_pe, 4)
            dve.wait_ge(f_got, 16)
            dve.wait_ge(e_applied, GROUPS)
            c.link(v.tensor_tensor(y[:, 0, 0:D], x1c[:, :], bank[7][:, 0:D], ALU.add))
            c.link(v.bn_stats(yst[:, 0, :], y[:, 0, 0:D]))
            v.bn_aggr(ymv[:, 0, 0, :], yst[:, 0, :]).then_inc(f_dve, 1)
            dve.wait_ge(f_act, 2)
            c.link(v.reciprocal(ysc[:, 0, 0, 0:1], ystd[:, 0, 0:1]))
            v.scalar_tensor_tensor(ysc[:, 0, 1, 0:1], ymv[:, 0, 0, 0:1], -1.0, ysc[:, 0, 0, 0:1], ALU.mult, ALU.mult)\
                .then_inc(f_dve, 1)


_INS = ["x", "src", "dst", "edge_attr_64", "L0_gnn_Wq", "L0_gnn_bq", "L0_gnn_Wk", "L0_gnn_bk", "L0_gnn_Wv",
        "L0_gnn_bv", "L0_gnn_Wb", "L0_gnn_bb", "L0_gnn_Wo", "L0_gnn_bo", "L1_gnn_W", "L1_gnn_a"]


def kernel(**inputs):
    import numpy as np
    import concourse.bacc as bacc
    from concourse import mybir as mb
    from concourse.bass_utils import run_bass_kernel_spmd

    nc = bacc.Bacc("TRN2", target_bir_lowering=False, num_devices=1)
    arrays, args = {}, []
    for name in _INS:
        a = np.ascontiguousarray(inputs[name])
        arrays[f"in_{name}"] = a
        args.append(nc.dram_tensor(f"in_{name}", a.shape, mb.dt.from_np(a.dtype), kind="ExternalInput").ap())
    args.append(nc.dram_tensor("out_dram", inputs["x"].shape, mb.dt.float32, kind="ExternalOutput").ap())
    gnn_kernel(nc, *args)
    return run_bass_kernel_spmd(nc, [arrays], core_ids=[0]).results[0]["out_dram"]
```

```python
import concourse.bass as bass
from concourse import mybir
from contextlib import ExitStack


UNROLL = 4


class Step:

    def __init__(self, off, i=None):
        self.off, self.i = off, i
        self.u, self.w = off % 2, off % 4
        self.g = off if i is None else i * UNROLL + off

    def uses(self, ring):
        count = self.off // ring + 1
        return count if self.i is None else self.i * (UNROLL // ring) + count

    def back(self, k):
        return Step(self.off - k, self.i)

    def runs(self, groups):
        return self.i is not None or 0 <= self.off < groups


def gnn_kernel(nc, x, src, dst, edge_attr, Wq, bq, Wk, bk, Wv, bv, Wb, bb, Wo, bo, W1, a1, out):
    fp32 = mybir.dt.float32
    i32 = mybir.dt.int32
    bf16 = mybir.dt.bfloat16
    ALU = mybir.AluOpType
    ACT = mybir.ActivationFunctionType
    AX = mybir.AxisListType.X

    P = 128
    N, D = x.shape
    NE = src.shape[0]
    ED = edge_attr.shape[1]
    H = 8
    HD = D // H
    G = 4
    TILES = -(-NE // (P * G)) * G
    GROUPS = TILES // G
    EP = P * TILES
    LASTROW = NE - (P - 1) * TILES
    ROWS = (N // P // (GROUPS - 1))
    MAIN = P * ROWS * (GROUPS - 1)
    REST = (N - MAIN) // ROWS
    PEEL = 9
    LOOPS = (GROUPS - PEEL) // UNROLL
    ATTR_PARTS = PEEL - 1
    ATTR_GROUPS = (GROUPS - PEEL) // ATTR_PARTS
    assert ATTR_GROUPS * ATTR_PARTS == GROUPS - PEEL
    assert (GROUPS - PEEL) % UNROLL == 0 and REST * ROWS == N - MAIN and REST <= P and 0 < LASTROW <= TILES
    GW = G * D
    BW = ROWS * D
    assert 2 * BW == 4 * GW
    EPS = 1e-5
    BIG = 1e30
    SKIP = 1e5
    SLOPE = 0.2
    CH = H * TILES

    xd_rows = nc.dram_tensor("xd_rows", (EP, D), fp32).ap()
    x1d_rows = nc.dram_tensor("x1d_rows", (EP, D), fp32).ap()
    v_rows = nc.dram_tensor("v_rows", (EP, D), fp32).ap()
    h_rows = nc.dram_tensor("h_rows", (EP, D), fp32).ap()
    x1_table = nc.dram_tensor("x1_table", (N, D), fp32).ap()
    dst_pad = nc.dram_tensor("dst_pad", (EP + 2,), i32)

    def edge_view(a):
        return a.rearrange("(p t) d -> p (t d)", p=P)

    def node_chunk(a, s):
        if s.i is None and s.off == 0:
            return a[MAIN:N, :].rearrange("(p r) d -> p (r d)", r=ROWS)
        return a[0:MAIN, :].rearrange("(p k) d -> p (k d)", p=P)[:, bass.ds((s.g - 1) * BW, BW)]

    def chunk_parts(s):
        return REST if s.i is None and s.off == 0 else P

    with ExitStack() as ctx:
        def sb(name, shape, dt=fp32):
            return ctx.enter_context(nc.sbuf_tensor(name, shape, dt))

        def sem(name):
            return ctx.enter_context(nc.semaphore(name))

        def sems(name, ring):
            return [sem(f"{name}{u}") for u in range(ring)]

        bank = [ctx.enter_context(nc.psum_tensor(f"bank{i}", [P, 512], fp32)) for i in range(8)]

        ident = sb("ident", [P, P])
        ones = sb("ones", [P, P])
        head_sel = sb("head_sel", [P, H])
        wq, wk, wv, wo, w1, w1T = (sb(n, [P, D]) for n in ("wq", "wk", "wv", "wo", "w1", "w1T"))
        bcol = sb("bcol", [P, 2])
        bb_col = sb("bb_col", [P, 1])
        wb_row = sb("wb_row", [P, ED])
        bias_rows = sb("bias_rows", [P, 2, D])
        bias_high, bias_mid = sb("bias_high", [P, 2, D], bf16), sb("bias_mid", [P, 2, D], bf16)
        bias_rest = sb("bias_rest", [P, 2, D])
        bias_parts = sb("bias_parts", [96, 2, D], bf16)
        ones_bf = sb("ones_bf", [96, P], bf16)
        bo_row = bias_rows[:, 1, :]
        a_col = sb("a_col", [P, 2])
        a_wide = sb("a_wide", [P, 2, P])
        v_src = sb("v_src", [P, D])
        v_dst = sb("v_dst", [P, D])

        sentinel = sb("sentinel", [1, 96], i32)
        src_tab = sb("src_tab", [P, TILES + 2 * G], i32)
        dst_raw = sb("dst_raw", [P, TILES + 2], i32)
        dst_f = sb("dst_f", [P, TILES + 2])
        dst_tab = sb("dst_tab", [P, TILES + 2 * G], i32)
        same_prev = sb("same_prev", [P, TILES])
        same_next = sb("same_next", [P, TILES])
        first = sb("first", [P, TILES])
        first_last = sb("first_last", [P, TILES])
        at_last_f = sb("at_last_f", [P, TILES])
        at_last2_f = sb("at_last2_f", [P, TILES])
        at_last = sb("at_last", [P, TILES + 2 * G], i32)
        at_last2 = sb("at_last2", [P, TILES + 2 * G], i32)
        carry_idx_f = sb("carry_idx_f", [P, 4])
        carry_idx = sb("carry_idx", [P, 2], i32)
        pen_local = sb("pen_local", [P, H, TILES])
        pen_first = sb("pen_first", [P, TILES])
        pen_pad = sb("pen_pad", [P, TILES])

        edge_in = sb("edge_in", [P, TILES * ED])
        edge_mul = sb("edge_mul", [P, G * ED])
        edge_bias = sb("edge_bias", [P, 4, 2, G])
        idx_slot = sb("idx_slot", [P, 4, 2 * G], i32)
        xs = sb("xs", [P, 4, GW])
        xd = sb("xd", [P, 4, GW])
        xsT = sb("xsT", [P, 2, GW])
        xdT = sb("xdT", [P, 2, GW])
        qT = sb("qT", [P, GW])
        prodT = sb("prodT", [P, 2, GW])
        node_in = sb("node_in", [P, 2, BW])
        node_x1 = sb("node_x1", [P, 2, BW])
        node_out = sb("node_out", [P, 2, BW])
        nst = sb("nst", [P, ROWS, 6])
        nmv = sb("nmv", [P, 2, ROWS, 2])
        nstd = sb("nstd", [P, 2, 2, ROWS])
        nsc = sb("nsc", [P, 4, 4, ROWS])
        eps_cols = sb("eps_cols", [P, 2])

        score = sb("score", [P, H, TILES])
        run_max = sb("run_max", [P, H, TILES])
        tmp = sb("tmp", [P, H, TILES])
        weight = sb("weight", [P, H, TILES])
        decay = sb("decay", [P, H, TILES])
        run_sum = sb("run_sum", [P, H, TILES])
        share = sb("share", [P, 2, 2, G * H])
        table_cell = sb("table_cell", [P, 1])
        ends = sb("ends", [P, 2, H])
        end_args = sb("end_args", [P, 2, H])
        factor_row = sb("factor_row", [H, P])
        carry_row = sb("carry_row", [H, 2, P + 1])
        carry_in = sb("carry_in", [P, 2, H])

        y = sb("y", [P, 2, GW])
        res = sb("res", [P, 4, GW])
        dots = sb("dots", [P, GW])
        dot4 = sb("dot4", [P, 4, G])
        yst = sb("yst", [P, G, 6])
        ymv = sb("ymv", [P, 2, G, 2])
        ystd = sb("ystd", [P, 2, G])
        ysc = sb("ysc", [P, 2, 2, G])

        s_src = sb("s_src", [P, TILES])
        s_dst = sb("s_dst", [P, TILES])
        logit = sb("logit", [P, TILES])
        logit2 = sb("logit2", [P, TILES])
        att = sb("att", [P, TILES])
        max_p = sb("max_p", [P, 1])
        max_all = sb("max_all", [1, 1])
        neg_max = sb("neg_max", [P, 1])
        exp_sum = sb("exp_sum", [P, 1])
        inv_sum = sb("inv_sum", [P, 1])
        hv, hT, xa, agg = (edge_in[:, k * 2 * GW:(k + 1) * 2 * GW].rearrange("p (u w) -> p u w", u=2)
                           for k in range(4))
        v_out, v_in, h_out = y, xs, xd
        h_in, x1d_in = (a[:, :, :].rearrange("p u (k w) -> p (u k) w", w=GW) for a in (node_x1, node_in))
        part = sb("part", [P, D])
        diag = sb("diag", [P, P])
        chunkrow = sb("chunkrow", [P, P])
        carryT = sb("carryT", [P, P + 1])
        total = sb("total", [P, D])
        x1c = sb("x1c", [P, D])

        consts_in = sem("consts_in")
        pad_in = sem("pad_in")
        edges_in = sem("edges_in")
        lists_in = sem("lists_in")
        attr_zeroed, attr_head, attr_in = sem("attr_zeroed"), sem("attr_head"), sem("attr_in")
        zeroed = sem("zeroed")
        built = sem("built")
        prep, prep_chain, last_chain = sem("prep"), sem("prep_chain"), sem("last_chain")
        w1T_done, w1T_sb = sem("w1T_done"), sem("w1T_sb")
        v_done = sem("v_done")
        held_pool, held_dve = sem("held_pool"), sem("held_dve")
        idx_ready = sem("idx_ready")
        got_src, got_dst = sems("got_src", 4), sems("got_dst", 4)
        xT_done, xT_sb = sem("xT_done"), sem("xT_sb")
        qk_done, q_sb = sem("qk_done"), sem("q_sb")
        prod_done, s_done, score_done = sem("prod_done"), sem("s_done"), sem("score_done")
        xd_stored, v_stored = sems("xd_stored", 4), sems("v_stored", 2)
        v_mm, v_sb = sem("v_mm"), sem("v_sb")
        node_twice, bias_ready = sem("node_twice"), sem("bias_ready")
        bias_chain, node_chain = sem("bias_chain"), sem("node_chain")
        node_loaded = sems("node_loaded", 2)
        node_var, node_std, node_ready, node_applied = (
            sem("node_var"), sem("node_std"), sem("node_ready"), sem("node_applied"))
        x1_stored, out_stored = sems("x1_stored", 2), sems("out_stored", 2)
        soft_chain, ends_ready, ends_T = sem("soft_chain"), sem("ends_ready"), sem("ends_T")
        row_ready, carry_T = sem("row_ready"), sem("carry_T")
        args_ready, exps_done = sem("args_ready"), sem("exps_done")
        sums_done = sem("sums_done")
        xd_back, v_back = sems("xd_back", 4), sems("v_back", 4)
        share_chain, share_ready = sem("share_chain"), sem("share_ready")
        hv_done, hv_T, hv_Tsb, o_mm = sem("hv_done"), sem("hv_T"), sem("hv_Tsb"), sem("o_mm")
        c_var, c_std = sem("c_var"), sem("c_std")
        c_fin_chain, node_fin_chain = sem("c_fin_chain"), sem("node_fin_chain")
        e_var, e_std, e_fin_chain = sem("e_var"), sem("e_std"), sem("e_fin_chain")
        c_chain, c_stats, c_applied, sd_chain, sd_done = (
            sem("c_chain"), sem("c_stats"), sem("c_applied"), sem("sd_chain"), sem("sd_done"))
        c_y = sem("c_y")
        c_scat, x1d_stored = sems("c_scat", 4), sems("x1d_stored", 4)
        d_idx, d_got, d_chain, d_done = sem("d_idx"), sems("d_got", 4), sem("d_chain"), sem("d_done")
        d_T, d_Tsb, h_mm, h_sb, h_stored = sem("d_T"), sem("d_Tsb"), sem("h_mm"), sem("h_sb"), sems("h_stored", 4)
        att_chain, max_col, max_T, max_one, max_b = (
            sem("att_chain"), sem("max_col"), sem("max_T"), sem("max_one"), sem("max_b"))
        neg_ready, exp_done, sum_b, att_ready = sem("neg_ready"), sem("exp_done"), sem("sum_b"), sem("att_ready")
        h_back, x1d_back = sems("h_back", 4), sems("x1d_back", 4)
        xa_done, r_chain, own_chain = sem("xa_done"), sem("r_chain"), sem("own_chain")
        e_y, e_chain, e_stats, e_applied = sem("e_y"), sem("e_chain"), sem("e_stats"), sem("e_applied")
        e_scat = sems("e_scat", 4)
        f_dve, f_pe, f_act, f_got, f_scat = sem("f_dve"), sem("f_pe"), sem("f_act"), sem("f_got"), sem("f_scat")

        block = ctx.enter_context(nc.Block())

        def wait(eng, s, value):
            if not isinstance(value, int) or value > 0:
                eng.wait_ge(s, value)

        def hold(eng, s, value):
            wait(eng, s, value)
            if not isinstance(value, int):
                eng.sem_inc(held_pool if eng is nc.gpsimd else held_dve, 1)

        def pipeline(eng, body, tail=0, apart=0):
            for g in range(PEEL):
                body(Step(g))
            with eng.Fori(0, LOOPS - apart // UNROLL, 1) as i:
                for off in range(PEEL, PEEL + UNROLL):
                    body(Step(off, i))
            for g in range(GROUPS - apart, GROUPS + tail):
                body(Step(g))

        class Chain:

            def __init__(self, eng, s, per_step, step=None):
                self.eng, self.sem, self.per, self.k = eng, s, per_step, 0
                self.base = 0 if step is None else step.g * per_step

            def put(self, ins):
                self.k += 1
                assert self.per is None or self.k <= self.per
                ins.then_inc(self.sem, 1)
                return self.k

            def see(self, k):
                hold(self.eng, self.sem, self.base + k)

            def link(self, ins):
                self.see(self.put(ins))

        T = lambda a, u, t: a[:, u, t * D:(t + 1) * D]

        def all_done(eng, sems, each):
            for k, s in enumerate(sems):
                eng.wait_ge(s, 16 * each * ((GROUPS - 1 - k) // len(sems) + 1))

        @block.sync
        def _(sp):
            head = 112
            sp.wait_ge(zeroed, 1)
            for tab, ends_of in ((src_tab, src), (dst_tab, dst)):
                sp.dma_start(tab[0:head, 0:TILES], ends_of[0:head * TILES].rearrange("(p t) -> p t", p=head))\
                    .then_inc(lists_in, 16)
                sp.dma_start(tab[head:P - 1, 0:TILES],
                             ends_of[head * TILES:(P - 1) * TILES].rearrange("(p t) -> p t", t=TILES))\
                    .then_inc(lists_in, 16)
                sp.dma_start(tab[P - 1:P, 0:LASTROW],
                             ends_of[(P - 1) * TILES:NE].rearrange("(p t) -> p t", p=1)).then_inc(lists_in, 16)
            sp.dma_start(dst_pad[0:1].rearrange("(a b) -> a b", a=1), sentinel[0:1, 0:1]).then_inc(pad_in, 16)
            sp.dma_start(dst_pad[NE + 1:EP + 2].rearrange("(a b) -> a b", a=1),
                         sentinel[0:1, 1:EP + 2 - NE]).then_inc(pad_in, 16)
            sp.dma_start(dst_pad[1:NE + 1].rearrange("(a b) -> a b", a=8),
                         dst.rearrange("(a b) -> a b", a=8)).then_inc(pad_in, 16)
            for tile, w in ((wq, Wq), (wk, Wk), (wv, Wv), (wo, Wo), (w1, W1)):
                sp.dma_start(tile[:, :], w).then_inc(consts_in, 16)
            for c, b in enumerate((bq, bk)):
                sp.dma_start(bcol[:, c:c + 1], b.rearrange("(p a) -> p a", a=1)).then_inc(consts_in, 16)
            sp.dma_start(bb_col[:, :], bb.rearrange("(p a) -> p a", a=1).to_broadcast([P, 1])).then_inc(consts_in, 16)
            sp.dma_start(wb_row[:, :], Wb.rearrange("e a -> a e").to_broadcast([P, ED])).then_inc(consts_in, 16)
            for c, b in enumerate((bv, bo)):
                sp.dma_start(bias_rows[:, c, :], b.rearrange("(a d) -> a d", a=1).to_broadcast([P, D]))\
                    .then_inc(consts_in, 16)
            for c in range(2):
                sp.dma_start(a_col[:, c:c + 1], a1[c * D:(c + 1) * D, :]).then_inc(consts_in, 16)
            sp.wait_ge(pad_in, 48)
            sp.dma_start(dst_raw[:, :], bass.AP(dst_pad, 0, [[TILES, P], [1, TILES + 2]])).then_inc(edges_in, 16)
            sp.wait_ge(attr_zeroed, 1)

            def load_attributes(group, groups, done):
                cols = slice(group * G * ED, (group + groups) * G * ED)
                rows = edge_attr[0:(P - 1) * TILES, :].rearrange("(p t) e -> p (t e)", t=TILES)
                sp.dma_start(edge_in[0:head, cols], rows[0:head, cols]).then_inc(done, 16)
                sp.dma_start(edge_in[head:P - 1, cols], rows[head:P - 1, cols]).then_inc(done, 16)
                cols = slice(cols.start, min(cols.stop, LASTROW * ED))
                if cols.start < cols.stop:
                    last_row = edge_attr[(P - 1) * TILES:NE, :].rearrange("(p t) e -> p (t e)", p=1)
                    sp.dma_start(edge_in[P - 1:P, cols], last_row[:, cols]).then_inc(done, 16)
            load_attributes(0, PEEL, attr_head)

            def stage2(s):
                if s.runs(GROUPS):
                    wait(sp, node_applied, s.g - 1)
                    sp.dma_start(node_in[0:chunk_parts(s), s.u, :], node_chunk(x, s)).then_inc(node_loaded[s.u], 16)
                if s.i is None and s.off < ATTR_PARTS:
                    load_attributes(PEEL + s.off * ATTR_GROUPS, ATTR_GROUPS, attr_in)
                b = s.back(1)
                if b.runs(GROUPS):
                    wait(sp, got_dst[b.w], b.uses(4) * 16 * G)
                    sp.dma_start(edge_view(xd_rows)[:, bass.ds(b.g * GW, GW)], xd[:, b.w, :])\
                        .then_inc(xd_stored[b.w], 16)
                b = s.back(2)
                if b.runs(GROUPS):
                    n = chunk_parts(b)
                    wait(sp, v_sb, b.g + 1)
                    sp.dma_start(edge_view(v_rows)[:, bass.ds(b.g * GW, GW)], v_out[:, b.u, :])\
                        .then_inc(v_stored[b.u], 16)
                    wait(sp, node_applied, b.g + 1)
                    sp.dma_start(node_chunk(x1_table, b), node_x1[0:n, b.u, :]).then_inc(x1_stored[b.u], 16)
                b = s.back(3)
                if b.runs(GROUPS):
                    n = chunk_parts(b)
                    wait(sp, node_twice, b.g + 1)
                    sp.dma_start(node_chunk(out, b), node_out[0:n, b.u, :]).then_inc(out_stored[b.u], 16)
            pipeline(sp, stage2, 3)
            all_done(sp, xd_stored, 1)
            all_done(sp, v_stored, 1)

            def stage4(s):
                if s.runs(GROUPS):
                    wait(sp, c_y, s.g - 3)
                    sp.dma_start(xd[:, s.w, :], edge_view(xd_rows)[:, bass.ds(s.g * GW, GW)]).then_inc(xd_back[s.w], 16)
                    wait(sp, hv_done, s.g - 3)
                    sp.dma_start(v_in[:, s.w, :], edge_view(v_rows)[:, bass.ds(s.g * GW, GW)]).then_inc(v_back[s.w], 16)
                b = s.back(5)
                if b.runs(GROUPS):
                    wait(sp, c_applied, b.g + 1)
                    sp.dma_start(edge_view(x1d_rows)[:, bass.ds(b.g * GW, GW)], res[:, b.w, :])\
                        .then_inc(x1d_stored[b.w], 16)
            sp.wait_ge(score_done, GROUPS)
            pipeline(sp, stage4, 5)

            def stage5(s):
                b = s.back(2)
                if b.runs(GROUPS):
                    wait(sp, h_sb, b.g + 1)
                    sp.dma_start(edge_view(h_rows)[:, bass.ds(b.g * GW, GW)], h_out[:, b.w, :])\
                        .then_inc(h_stored[b.w], 16)
            def load_h(s):
                sp.dma_start(h_in[:, s.w, :], edge_view(h_rows)[:, bass.ds(s.g * GW, GW)]).then_inc(h_back[s.w], 16)

            def load_x1d(s):
                sp.dma_start(x1d_in[:, s.w, :], edge_view(x1d_rows)[:, bass.ds(s.g * GW, GW)])\
                    .then_inc(x1d_back[s.w], 16)

            pipeline(sp, stage5)
            all_done(sp, x1d_stored, 1)
            for g in range(4):
                sp.wait_ge(h_stored[g], 16)
                load_h(Step(g))
                load_x1d(Step(g))
            for g in range(GROUPS, GROUPS + 2):
                stage5(Step(g))
            all_done(sp, h_stored, 1)

            def stage7(s):
                if s.i is not None or s.off >= 4:
                    wait(sp, xa_done, s.g - 3)
                    load_h(s)
                    wait(sp, e_y, s.g - 3)
                    load_x1d(s)
            pipeline(sp, stage7)
            all_done(sp, out_stored, 1)
            all_done(sp, e_scat, G)
            sp.wait_ge(f_scat, 16)

        @block.gpsimd
        def _(pool):
            pool.memset(sentinel[:, :], N).then_inc(built, 1)
            pool.memset(src_tab[:, :], 0)
            pool.memset(dst_tab[:, :], 0)
            pool.wait_ge(built, 1)
            pool.memset(sentinel[:, 0:1], -1).then_inc(zeroed, 1)
            pool.memset(ident[:, :], 0.0)
            pool.memset(head_sel[:, :], 1.0).then_inc(built, 1)
            pool.wait_ge(built, 2)
            pool.affine_select(out=ident[:, :], in_=ident[:, :], compare_op=ALU.not_equal, fill=1.0,
                               base=0, pattern=[[-1, P]], channel_multiplier=1)
            pool.affine_select(out=head_sel[:, :], in_=head_sel[:, :], compare_op=ALU.is_ge, fill=0.0,
                               base=0, pattern=[[-HD, H]], channel_multiplier=1).then_inc(built, 1)
            pool.wait_ge(built, 3)
            pool.affine_select(out=head_sel[:, :], in_=head_sel[:, :], compare_op=ALU.is_ge, fill=0.0,
                               base=HD - 1, pattern=[[HD, H]], channel_multiplier=-1).then_inc(built, 1)

            def rows(tile, u, t):
                return tile[:, u, t * D:(t + 1) * D]

            def gather(tile, table, idx, u, t, done):
                pool.indirect_dma_start(out=rows(tile, u, t), out_offset=None, in_=table,
                                        in_offset=bass.IndirectOffsetOnAxis(ap=idx, axis=0))\
                    .then_inc(done, 16)

            def scatter(table, tile, idx, u, t, done):
                pool.indirect_dma_start(out=table, out_offset=bass.IndirectOffsetOnAxis(ap=idx, axis=0),
                                        in_=rows(tile, u, t), in_offset=None,
                                        bounds_check=N - 1, oob_is_err=False).then_inc(done, 16)

            def stage2(s):
                hold(pool, idx_ready, s.g + 1)
                hold(pool, xT_done, s.g - 3)
                for t in range(G):
                    gather(xs, x, idx_slot[:, s.w, t:t + 1], s.w, t, got_src[s.w])
                hold(pool, xd_stored[s.w], s.back(4).uses(4) * 16)
                for t in range(G):
                    gather(xd, x, idx_slot[:, s.w, G + t:G + t + 1], s.w, t, got_dst[s.w])
            pipeline(pool, stage2)
            all_done(pool, x1_stored, 1)

            def stage4(s):
                hold(pool, c_applied, s.g + 1)
                for t in range(G):
                    scatter(x1_table, res, idx_slot[:, s.w, t:t + 1], s.w, t, c_scat[s.w])
            pipeline(pool, stage4)
            all_done(pool, c_scat, G)

            def stage5(s):
                hold(pool, d_idx, s.g + 1)
                hold(pool, d_done, s.g - 3)
                hold(pool, d_T, s.g - 3)
                for t in range(G):
                    gather(xs, x1_table, idx_slot[:, s.w, t:t + 1], s.w, t, d_got[s.w])
            pipeline(pool, stage5)
            gather_c = pool.indirect_dma_start(out=x1c[:, :], out_offset=None, in_=x1_table,
                                               in_offset=bass.IndirectOffsetOnAxis(ap=carry_idx[:, 0:1], axis=0))
            gather_c.then_inc(f_got, 16)
            all_done(pool, out_stored, 1)

            def stage7(s):
                hold(pool, e_applied, s.g + 1)
                for t in range(G):
                    scatter(out, res, idx_slot[:, s.w, t:t + 1], s.w, t, e_scat[s.w])
            pipeline(pool, stage7)
            pool.wait_ge(f_act, 2)
            pool.indirect_dma_start(out=out, out_offset=bass.IndirectOffsetOnAxis(ap=carry_idx[:, 1:2], axis=0),
                                    in_=total[:, :], in_offset=None,
                                    bounds_check=N - 1, oob_is_err=False).then_inc(f_scat, 16)

        @block.tensor
        def _(pe):
            mm, tr = nc.tensor.matmul, nc.tensor.transpose
            pe.wait_ge(consts_in, 16 * 13)
            pe.wait_ge(built, 4)
            tr(bank[0][:, 0:P], w1[:, :], ident[:, :]).then_inc(w1T_done, 1)
            pe.wait_ge(w1T_sb, 1)
            pe.wait_ge(prep, 1)
            for c in range(2):
                last = mm(bank[1][:, c * D:(c + 1) * D], a_wide[:, c, :], w1T[:, :], start=True, stop=True)
            last.then_inc(v_done, 1)

            def add_bias(to, k):
                mm(to[:, :], ones_bf[:, :], bias_parts[:, k, :].unsqueeze(1).to_broadcast([96, G, D]),
                   start=True, stop=False)

            def stage2(s):
                d, b = s.back(2), s.back(1)
                if d.runs(GROUPS):
                    wait(pe, prod_done, d.g + 1)
                    wait(pe, score_done, d.g - 1)
                    for t in range(G):
                        last = mm(bank[6 + d.u][:, t * H:(t + 1) * H], prodT[:, d.u, t * P:(t + 1) * P],
                                  head_sel[:, :], start=True, stop=True)
                    last.then_inc(s_done, 1)
                if b.runs(GROUPS):
                    wait(pe, xT_sb, b.g * 2 + 2)
                    wait(pe, q_sb, b.g)
                    wait(pe, prod_done, b.g)
                    mm(bank[4][:, :], wq[:, :], xsT[:, b.u, :], start=True, stop=True)
                    mm(bank[5][:, :], wk[:, :], xdT[:, b.u, :], start=True, stop=True).then_inc(qk_done, 1)
                    wait(pe, v_sb, b.g - 1)
                    add_bias(bank[b.u], 0)
                    for t in range(G):
                        last = mm(bank[b.u][:, t * D:(t + 1) * D], T(xdT, b.u, t), wv[:, :], start=False,
                                  stop=t == G - 1)
                    last.then_inc(v_mm, 1)
                if s.runs(GROUPS):
                    wait(pe, xT_sb, s.g * 2)
                    wait(pe, got_src[s.w], s.uses(4) * 16 * G)
                    for t in range(G):
                        tr(bank[2][:, t * P:(t + 1) * P], T(xs, s.w, t), ident[:, :])
                    wait(pe, got_dst[s.w], s.uses(4) * 16 * G)
                    for t in range(G):
                        last = tr(bank[3][:, t * P:(t + 1) * P], T(xd, s.w, t), ident[:, :])
                    last.then_inc(xT_done, 1)
            pe.wait_ge(prep, 2)
            pipeline(pe, stage2, 2)

            pe.wait_ge(v_sb, GROUPS)
            for k in range(2):
                pe.wait_ge(ends_ready, k + 1)
                tr(bank[0][0:H, 0:P], ends[:, 0, :], ident[:, :])
                tr(bank[0][0:H, P:2 * P], ends[:, 1, :], ident[:, :]).then_inc(ends_T, 1)
                pe.wait_ge(row_ready, k + 1)
                tr(bank[1][:, 0:H], carry_row[:, k, 0:P], ident[0:H, 0:H]).then_inc(carry_T, 1)

            def stage4(s):
                if s.runs(GROUPS):
                    wait(pe, hv_done, s.g + 1)
                    wait(pe, hv_Tsb, s.g - 1)
                    for t in range(G):
                        last = tr(bank[2 + s.u][:, t * P:(t + 1) * P], T(hv, s.u, t), ident[:, :])
                    last.then_inc(hv_T, 1)
                b = s.back(1)
                if b.runs(GROUPS):
                    wait(pe, hv_Tsb, b.g + 1)
                    wait(pe, c_y, b.g - 1)
                    add_bias(bank[b.u], 1)
                    for t in range(G):
                        last = mm(bank[b.u][:, t * D:(t + 1) * D], T(hT, b.u, t), wo[:, :], start=False,
                                  stop=t == G - 1)
                    last.then_inc(o_mm, 1)
            pe.wait_ge(sums_done, 1)
            pipeline(pe, stage4, 1)

            def stage5(s):
                b = s.back(1)
                if b.runs(GROUPS):
                    wait(pe, d_Tsb, b.g + 1)
                    wait(pe, h_sb, b.g - 1)
                    for t in range(G):
                        last = mm(bank[4 + b.u][:, t * D:(t + 1) * D], T(xsT, b.u, t), w1[:, :], start=True, stop=True)
                    last.then_inc(h_mm, 1)
                if s.runs(GROUPS):
                    wait(pe, d_got[s.w], s.uses(4) * 16 * G)
                    wait(pe, d_Tsb, s.g - 1)
                    for t in range(G):
                        last = tr(bank[6 + s.u][:, t * P:(t + 1) * P], T(xs, s.w, t), ident[:, :])
                    last.then_inc(d_T, 1)
            pipeline(pe, stage5, 1)

            pe.wait_ge(max_col, 1)
            tr(bank[2][0:1, 0:P], max_p[:, :], ident[:, :]).then_inc(max_T, 1)
            pe.wait_ge(max_one, 1)
            mm(bank[3][:, 0:1], ones[0:1, :], max_all[:, :], start=True, stop=True).then_inc(max_b, 1)
            pe.wait_ge(exp_done, 1)
            mm(bank[4][:, 0:1], ones[:, :], exp_sum[:, :], start=True, stop=True)
            mm(bank[5][:, 0:P], ones[:, :], diag[:, :], start=True, stop=True).then_inc(sum_b, 1)
            pe.wait_ge(att_ready, 1)

            def stage7(s):
                wait(pe, x1d_back[s.w], s.uses(4) * 16)
                wait(pe, e_applied, s.g - 3)
                mm(bank[s.w][:, :], ident[:, :], x1d_in[:, s.w, :], start=True, stop=False)
                wait(pe, r_chain, (s.g + 1) * G)
                mm(bank[s.w][:, :], ident[:, :], agg[:, s.u, :], start=False, stop=True).then_inc(e_y, 1)
            pipeline(pe, stage7)
            tr(bank[4][:, 0:P], T(agg, (GROUPS - 1) % 2, G - 1), ident[:, :]).then_inc(f_pe, 1)
            pe.wait_ge(f_dve, 1)
            tr(bank[5][:, 0:P], carryT[:, 0:P], ident[:, :]).then_inc(f_pe, 1)

        @block.scalar
        def _(act):
            fn = nc.scalar.activation
            act.wait_ge(w1T_done, 1)
            fn(w1T[:, :], bank[0][:, 0:P], ACT.Copy).then_inc(w1T_sb, 1)

            def stage2(s):
                b = s.back(1)
                if b.runs(GROUPS):
                    n = chunk_parts(b)
                    wait(act, node_var, b.g + 1)
                    wait(act, node_ready, b.g - 1)
                    var = nmv[0:n, b.u, :, 1]
                    fn(nstd[0:n, b.u, 0, :], var, ACT.Sqrt, bias=eps_cols[0:n, 0:1])
                    fn(nstd[0:n, b.u, 1, :], var, ACT.Sqrt, bias=eps_cols[0:n, 1:2], scale=1.0 + EPS)\
                        .then_inc(node_std, 1)

                def transposes():
                    wait(act, xT_done, s.g + 1)
                    wait(act, v_mm, s.g - 1)
                    fn(xsT[:, s.u, :], bank[2][:, :], ACT.Copy).then_inc(xT_sb, 1)
                    fn(xdT[:, s.u, :], bank[3][:, :], ACT.Copy).then_inc(xT_sb, 1)

                if b.runs(GROUPS):
                    wait(act, qk_done, b.g + 1)
                    wait(act, prod_done, b.g)
                    fn(qT[:, :], bank[4][:, :], ACT.Identity, bias=bcol[:, 0:1]).then_inc(q_sb, 1)
                    if s.i is None and s.g == GROUPS - 1:
                        transposes()
                    wait(act, node_ready, b.g + 1)
                    wait(act, x1_stored[b.u], b.back(2).uses(2) * 16)
                    wait(act, node_twice, b.g - 1)
                    for r in range(ROWS):
                        cols = slice(r * D, (r + 1) * D)
                        last = fn(node_x1[0:n, b.u, cols], node_in[0:n, b.u, cols], ACT.Identity,
                                  bias=nsc[0:n, b.w, 2, r:r + 1], scale=nsc[0:n, b.w, 0, r:r + 1])
                    last.then_inc(node_applied, 1)
                    wait(act, v_mm, b.g + 1)
                    wait(act, v_stored[b.u], b.back(2).uses(2) * 16)
                    fn(v_out[:, b.u, :], bank[b.u][:, :], ACT.Copy).then_inc(v_sb, 1)
                if s.runs(GROUPS) and not (s.i is None and s.g == GROUPS - 1):
                    transposes()
            act.wait_ge(consts_in, 16 * 13)
            pipeline(act, stage2, 1, UNROLL)

            for k, e in enumerate((weight, decay)):
                act.wait_ge(args_ready, k + 1)
                fn(e[:, :, :], e[:, :, :], ACT.Exp).then_inc(exps_done, 1)
            act.wait_ge(args_ready, 3)
            fn(ends[:, 1, :], end_args[:, 1, :], ACT.Exp).then_inc(exps_done, 1)
            act.wait_ge(args_ready, 4)
            for h in range(H):
                last = fn(tmp[:, h, :], tmp[:, h, :], ACT.Exp, bias=carry_in[:, 0, h:h + 1])
            last.then_inc(exps_done, 1)
            fn(table_cell[:, :], eps_cols[:, 0:1], ACT.Sqrt)

            def apply(b, rows, stats, done, at, first_free):
                wait(act, stats, b.g + 1)
                first_free()
                fn(idx_slot[:, b.w, 0:G], at[:, bass.ds(b.g * G, G)], ACT.Copy)
                for t in range(G):
                    last = fn(T(res, b.w, t), rows[:, t * D:(t + 1) * D], ACT.Identity,
                              bias=ysc[:, b.u, 1, t:t + 1], scale=ysc[:, b.u, 0, t:t + 1])
                last.then_inc(done, 1)

            def deviation(b, var_ready, std_ready, stats):
                wait(act, var_ready, b.g + 1)
                wait(act, stats, b.g - 1)
                fn(ystd[:, b.u, :], ymv[:, b.u, :, 1], ACT.Sqrt, bias=eps_cols[:, 0:1]).then_inc(std_ready, 1)

            def stage4(s):
                b, a = s.back(3), s.back(1)
                if b.runs(GROUPS):
                    deviation(b, c_var, c_std, c_stats)
                if a.runs(GROUPS):
                    wait(act, hv_T, a.g + 1)
                    wait(act, o_mm, a.g - 1)
                    fn(hT[:, a.u, :], bank[2 + a.u][:, :], ACT.Copy).then_inc(hv_Tsb, 1)
                if b.runs(GROUPS):
                    def free():
                        wait(act, sd_done, b.g - 3)
                        wait(act, x1d_stored[b.w], b.back(4).uses(4) * 16)
                        wait(act, c_scat[b.w], b.back(4).uses(4) * 16 * G)
                    apply(b, y[:, b.u, :], c_stats, c_applied, at_last, free)
            pipeline(act, stage4, 3)

            fn(table_cell[:, :], eps_cols[:, 0:1], ACT.Exp)

            def stage5(s):
                b = s.back(1)
                if s.runs(GROUPS):
                    wait(act, d_T, s.g + 1)
                    wait(act, h_mm, s.g - 1)
                    fn(xsT[:, s.u, :], bank[6 + s.u][:, :], ACT.Copy).then_inc(d_Tsb, 1)
                if b.runs(GROUPS):
                    wait(act, h_mm, b.g + 1)
                    wait(act, h_stored[b.w], b.back(4).uses(4) * 16)
                    fn(h_out[:, b.w, :], bank[4 + b.u][:, :], ACT.Copy).then_inc(h_sb, 1)
            pipeline(act, stage5, 1)

            act.wait_ge(neg_ready, 1)
            fn(att[:, :], logit[:, :], ACT.Exp, bias=neg_max[:, :], accum_out=exp_sum[:, :]).then_inc(exp_done, 1)
            fn(table_cell[:, :], eps_cols[:, 0:1], ACT.Sqrt)
            act.wait_ge(att_ready, 1)
            all_done(act, x1d_stored, 1)
            all_done(act, c_scat, G)

            def stage7(s):
                b = s.back(3)
                if s.runs(GROUPS):
                    wait(act, h_back[s.w], s.uses(4) * 16)
                    wait(act, r_chain, (s.g - 1) * G)
                    for t in range(G):
                        last = fn(T(xa, s.u, t), T(h_in, s.w, t), ACT.Copy, scale=att[:, bass.ds(s.g * G + t, 1)])
                    last.then_inc(xa_done, 1)
                if b.runs(GROUPS):
                    deviation(b, e_var, e_std, e_stats)
                    apply(b, bank[b.w], e_stats, e_applied, at_last2,
                          lambda: wait(act, e_scat[b.w], b.back(4).uses(4) * 16 * G))
            pipeline(act, stage7, 3)
            act.wait_ge(f_dve, 3)
            fn(ystd[:, 0, 0:1], ymv[:, 0, 0, 1:2], ACT.Sqrt, bias=eps_cols[:, 0:1]).then_inc(f_act, 1)
            act.wait_ge(f_dve, 4)
            fn(total[:, :], y[:, 0, 0:D], ACT.Identity, bias=ysc[:, 0, 1, 0:1], scale=ysc[:, 0, 0, 0:1])\
                .then_inc(f_act, 1)

        @block.vector
        def _(dve):
            v = nc.vector
            def fetch_indices(s, both, ready):
                at = bass.ds((s.g + 2) * G, G)
                w = (s.w + 2) % 4
                last = v.tensor_copy(idx_slot[:, w, 0:G], src_tab[:, at])
                if both:
                    last = v.tensor_copy(idx_slot[:, w, G:2 * G], dst_tab[:, at])
                last.then_inc(ready, 1)

            chain = Chain(dve, prep_chain, None)
            v.memset(edge_in[:, LASTROW * ED:TILES * ED], 0.0).then_inc(attr_zeroed, 1)
            v.memset(ones[:, :], 1.0)
            v.memset(eps_cols[:, 0:1], EPS)
            v.memset(eps_cols[:, 1:2], EPS * EPS)
            v.memset(part[:, :], 0.0)
            v.memset(carryT[:, 0:1], 0.0)
            v.memset(carry_row[:, 0, 0:1], -BIG)
            v.memset(decay[:, :, 0:1], -BIG)
            v.memset(carry_row[:, 1, 0:1], 0.0)
            dve.wait_ge(lists_in, 96)
            fetch_indices(Step(-2), True, idx_ready)
            fetch_indices(Step(-1), True, idx_ready)
            dve.wait_ge(consts_in, 16 * 13)
            for c in range(2):
                last = v.tensor_copy(a_wide[:, c, :], a_col[:, c:c + 1].to_broadcast([P, P]))
            last.then_inc(prep, 1)
            v.memset(bias_parts[:, :, :], 0.0)
            v.memset(ones_bf[:, :], 1.0)
            chain.link(v.tensor_copy(bias_high[:, :, :], bias_rows[:, :, :]))
            v.tensor_copy(bias_parts[0:1, :, :], bias_high[0:1, :, :])
            chain.link(v.tensor_tensor(bias_rest[:, :, :], bias_rows[:, :, :], bias_high[:, :, :], ALU.subtract))
            chain.link(v.tensor_copy(bias_mid[:, :, :], bias_rest[:, :, :]))
            v.tensor_copy(bias_parts[32:33, :, :], bias_mid[32:33, :, :])
            v.tensor_tensor(bias_parts[64:65, :, :], bias_rest[64:65, :, :], bias_mid[64:65, :, :], ALU.subtract)
            dve.wait_ge(edges_in, 16)
            chain.link(v.tensor_copy(dst_f[:, :], dst_raw[:, :]))
            cur, prv, nxt = dst_f[:, 1:TILES + 1], dst_f[:, 0:TILES], dst_f[:, 2:TILES + 2]
            v.tensor_tensor(same_prev[:, :], cur, prv, ALU.is_equal)
            v.tensor_tensor(same_next[:, :], cur, nxt, ALU.is_equal)
            v.tensor_scalar(pen_pad[:, :], cur, float(N), -BIG, ALU.is_ge, ALU.mult)
            chain.link(v.tensor_scalar(first[:, :], cur, dst_f[:, 0:1], None, ALU.is_equal))
            v.memset(same_prev[:, 0:1], 0.0)
            v.scalar_tensor_tensor(at_last_f[:, :], same_next[:, :], SKIP, cur, ALU.mult, ALU.add)
            v.tensor_scalar(pen_first[:, :], first[:, :], 1.0, BIG, ALU.subtract, ALU.mult)
            v.tensor_tensor(first_last[:, :], first[:, :], same_next[:, :], ALU.mult)
            v.tensor_scalar(carry_idx_f[:, 0:1], dst_f[:, 0:1], 0.0, float(N - 1), ALU.max, ALU.min)
            v.tensor_tensor(carry_idx_f[:, 2:3], dst_f[:, TILES + 1:TILES + 2], dst_f[:, 0:1], ALU.is_equal)
            dve.wait_ge(built, 4)
            chain.link(v.tensor_scalar(diag[:, :], ident[:, :], first[:, TILES - 1:TILES], None, ALU.mult))
            v.tensor_tensor(first_last[:, :], first[:, :], first_last[:, :], ALU.subtract)
            v.tensor_copy(at_last[:, 0:TILES], at_last_f[:, :])
            v.scalar_tensor_tensor(at_last2_f[:, :], first[:, :], SKIP, at_last_f[:, :], ALU.mult, ALU.add)
            v.tensor_copy(carry_idx[:, 0:1], carry_idx_f[:, 0:1])
            chain.link(v.tensor_tensor(carry_idx_f[:, 3:4], carry_idx_f[:, 2:3], first[:, 0:1], ALU.subtract))
            v.tensor_copy(at_last2[:, 0:TILES], at_last2_f[:, :])
            chain.link(v.tensor_scalar(carry_idx_f[:, 2:3], carry_idx_f[:, 3:4], 1.0, SKIP, ALU.add, ALU.mult))
            chain.link(v.tensor_tensor(carry_idx_f[:, 3:4], carry_idx_f[:, 2:3], dst_f[:, 0:1], ALU.add))
            v.tensor_copy(carry_idx[:, 1:2], carry_idx_f[:, 3:4])
            v.tensor_copy(ends[:, 1, :], pen_first[:, TILES - 1:TILES].to_broadcast([P, H]))
            v.tensor_scalar(pen_local[:, :, :], same_prev[:, :].unsqueeze(1).to_broadcast([P, H, TILES]),
                            1.0, BIG, ALU.subtract, ALU.mult)
            dve.wait_ge(v_done, 1)
            v.tensor_copy(v_src[:, :], bank[1][:, 0:D])
            v.tensor_copy(v_dst[:, :], bank[1][:, D:2 * D]).then_inc(prep, 1)

            attr_loads = sum(2 + ((PEEL + k * ATTR_GROUPS) * G < LASTROW) for k in range(ATTR_PARTS))

            def second_norm(d):
                nd = chunk_parts(d)
                rows = lambda a: a[0:nd, d.u, :].rearrange("p (r d) -> p r d", r=ROWS)
                wait(dve, node_applied, d.g + 1)
                wait(dve, out_stored[d.u], d.back(2).uses(2) * 16)
                v.tensor_tensor(rows(node_out), rows(node_x1),
                                nsc[0:nd, d.w, 3, :].unsqueeze(2).to_broadcast([nd, ROWS, D]), ALU.mult)\
                    .then_inc(node_twice, 1)

            def stage2(s):
                b, d = s.back(1), s.back(2)
                if b.runs(GROUPS):
                    nb = chunk_parts(b)
                    fin = Chain(dve, node_fin_chain, 1, b)
                    k = nsc[0:nb, b.w, :, :]
                    wait(dve, node_std, b.g + 1)
                    wait(dve, node_twice, b.g - 3)
                    inverse = fin.put(v.reciprocal(k[:, 0:2], nstd[0:nb, b.u, :, :]))
                    fin.see(inverse)
                    v.tensor_tensor(k[:, 3], nstd[0:nb, b.u, 0, :], k[:, 1], ALU.mult)
                    v.scalar_tensor_tensor(k[:, 2], nmv[0:nb, b.u, :, 0], -1.0, k[:, 0], ALU.mult, ALU.mult)\
                        .then_inc(node_ready, 1)
                if s.runs(GROUPS):
                    wait(dve, got_src[d.w], d.uses(4) * 16 * G)
                    wait(dve, got_dst[d.w], d.uses(4) * 16 * G)
                    fetch_indices(s, True, idx_ready)
                    n = chunk_parts(s)
                    ec, c = Chain(dve, bias_chain, 2, s), Chain(dve, node_chain, 2, s)
                    cols = bass.ds(s.g * G * ED, G * ED)
                    mul = edge_mul[:, :].rearrange("p (t e) -> p t e", t=G)
                    yv = node_in[0:n, s.u, :].rearrange("p (r d) -> p r d", r=ROWS)
                    if s.i is None and s.off == 0:
                        dve.wait_ge(attr_head, 48)
                    product = ec.put(v.tensor_tensor(mul, edge_in[:, cols].rearrange("p (t e) -> p t e", t=G),
                                                     wb_row[:, :].unsqueeze(1).to_broadcast([P, G, ED]), ALU.mult))
                    wait(dve, node_loaded[s.u], s.uses(2) * 16)
                    biased = c.put(v.tensor_tensor(yv, yv, bo_row[0:n, :].unsqueeze(1).to_broadcast([n, ROWS, D]),
                                                   ALU.add))
                    ec.see(product)
                    if s.i is None and s.off == PEEL - 1:
                        dve.wait_ge(attr_in, 16 * attr_loads)
                    total_e = ec.put(v.tensor_reduce(edge_bias[:, s.w, 0, :], mul, AX, ALU.add))
                    c.see(biased)
                    for r in range(ROWS):
                        last = v.bn_stats(nst[0:n, r, :], node_in[0:n, s.u, r * D:(r + 1) * D])
                    stats = c.put(last)
                if b.runs(GROUPS):
                    wait(dve, q_sb, b.g + 1)
                    wait(dve, s_done, b.g - 1)
                    v.scalar_tensor_tensor(prodT[:, b.u, :], bank[5][:, :], bcol[:, 1:2], qT[:, :],
                                           ALU.add, ALU.mult).then_inc(prod_done, 1)
                if s.runs(GROUPS):
                    ec.see(total_e)
                    v.tensor_scalar(edge_bias[:, s.w, 1, :], edge_bias[:, s.w, 0, :], bb_col[:, :], None, ALU.add)\
                        .then_inc(bias_ready, 1)
                if d.runs(GROUPS):
                    wait(dve, s_done, d.g + 1)
                    wait(dve, bias_ready, d.g + 1)
                    v.scalar_tensor_tensor(score[:, :, bass.ds(d.g * G, G)],
                                           bank[6 + d.u][:, 0:G * H].rearrange("p (t h) -> p h t", t=G),
                                           float(HD) ** -0.5,
                                           edge_bias[:, d.w, 1, :].unsqueeze(1).to_broadcast([P, H, G]),
                                           ALU.mult, ALU.add).then_inc(score_done, 1)
                if s.runs(GROUPS):
                    c.see(stats)
                    for r in range(ROWS):
                        last = v.bn_aggr(nmv[0:n, s.u, r, :], nst[0:n, r, :])
                    last.then_inc(node_var, 1)
                if d.runs(GROUPS) and (s.i is not None or s.g < GROUPS + 1):
                    second_norm(d)
            pipeline(dve, stage2, 2)

            flat = lambda a: a[:, :, :].rearrange("p h t -> p (h t)")
            c = Chain(dve, soft_chain, None)
            dve.wait_ge(score_done, GROUPS)
            c.link(v.tensor_tensor_scan(flat(run_max), flat(pen_local), flat(score), -BIG, ALU.add, ALU.max))
            v.tensor_copy(ends[:, 0, :], run_max[:, :, TILES - 1]).then_inc(ends_ready, 1)
            second_norm(Step(GROUPS - 1))
            dve.wait_ge(ends_T, 1)
            c.link(v.tensor_copy(factor_row[:, :], bank[0][0:H, P:2 * P]))
            v.tensor_tensor_scan(carry_row[:, 0, 1:P + 1], factor_row[:, :], bank[0][0:H, 0:P], -BIG,
                                 ALU.add, ALU.max).then_inc(row_ready, 1)
            dve.wait_ge(carry_T, 1)
            c.link(v.tensor_copy(carry_in[:, 0, :], bank[1][:, 0:H]))
            for h in range(H):
                last = v.scalar_tensor_tensor(run_max[:, h, :], pen_first[:, :], carry_in[:, 0, h:h + 1],
                                              run_max[:, h, :], ALU.add, ALU.max)
            c.link(last)
            v.tensor_tensor(end_args[:, 0, :], carry_in[:, 0, :], run_max[:, :, TILES - 1], ALU.subtract)
            v.tensor_tensor(weight[:, :, :], score[:, :, :], run_max[:, :, :], ALU.subtract).then_inc(args_ready, 1)
            c.link(v.tensor_tensor(decay[:, :, 1:TILES], run_max[:, :, 0:TILES - 1], run_max[:, :, 1:TILES],
                                   ALU.subtract))
            v.tensor_tensor(decay[:, :, 1:TILES], decay[:, :, 1:TILES], pen_local[:, :, 1:TILES], ALU.add)\
                .then_inc(args_ready, 1)
            v.tensor_scalar(end_args[:, 1, :], end_args[:, 0, :], pen_first[:, TILES - 1:TILES], None, ALU.add)\
                .then_inc(args_ready, 1)
            v.tensor_tensor(tmp[:, :, :], pen_first[:, :].unsqueeze(1).to_broadcast([P, H, TILES]), run_max[:, :, :],
                            ALU.subtract).then_inc(args_ready, 1)
            dve.wait_ge(exps_done, 2)
            c.link(v.tensor_tensor_scan(flat(run_sum), flat(decay), flat(weight), 0.0, ALU.mult, ALU.add))
            dve.wait_ge(exps_done, 3)
            v.tensor_copy(ends[:, 0, :], run_sum[:, :, TILES - 1]).then_inc(ends_ready, 1)
            dve.wait_ge(ends_T, 2)
            dve.wait_ge(exps_done, 4)
            c.link(v.tensor_copy(factor_row[:, :], bank[0][0:H, P:2 * P]))
            v.tensor_tensor_scan(carry_row[:, 1, 1:P + 1], factor_row[:, :], bank[0][0:H, 0:P], 0.0,
                                 ALU.mult, ALU.add).then_inc(row_ready, 1)
            dve.wait_ge(carry_T, 2)
            c.link(v.tensor_copy(carry_in[:, 1, :], bank[1][:, 0:H]))
            for h in range(H):
                last = v.scalar_tensor_tensor(run_sum[:, h, :], tmp[:, h, :], carry_in[:, 1, h:h + 1],
                                              run_sum[:, h, :], ALU.mult, ALU.add)
            last.then_inc(sums_done, 1)

            def invert(b, chain_sem, std_ready, applied):
                c = Chain(dve, chain_sem, 1, b)
                wait(dve, std_ready, b.g + 1)
                wait(dve, applied, b.g - 1)
                c.put(v.reciprocal(ysc[:, b.u, 0, :], ystd[:, b.u, :]))
                return c

            def shift(b, c, stats_done):
                c.see(1)
                v.scalar_tensor_tensor(ysc[:, b.u, 1, :], ymv[:, b.u, :, 0], -1.0, ysc[:, b.u, 0, :],
                                       ALU.mult, ALU.mult).then_inc(stats_done, 1)

            def moments(b, rows, tiles):
                for t in tiles:
                    last = v.bn_stats(yst[:, t, :], rows[:, t * D:(t + 1) * D])
                return last

            def combine(b, tiles):
                for t in tiles:
                    last = v.bn_aggr(ymv[:, b.u, t, :], yst[:, t, :])
                return last

            def dot(rows, vector, b, dot_sem):
                for t in range(G):
                    last = v.tensor_tensor_reduce(out=dots[:, t * D:(t + 1) * D], in0=T(rows, b.w, t), in1=vector[:, :],
                                                  scale=1.0, scalar=0.0, op0=ALU.mult, op1=ALU.add,
                                                  accum_out=dot4[:, b.w, t:t + 1])
                last.then_inc(dot_sem, 1)

            def keep_dots(scores, b, dot_sem, done):
                wait(dve, dot_sem, b.g + 1)
                v.tensor_copy(scores[:, bass.ds(b.g * G, G)], dot4[:, b.w, :]).then_inc(done, 1)

            def stage4(s):
                a, b, i, d = s.back(1), s.back(3), s.back(4), s.back(5)
                if s.runs(GROUPS):
                    sums = run_sum[:, :, bass.ds(s.g * G, G)]
                    step_of = lambda k: share[:, s.u, k, :].rearrange("p (t h) -> p h t", t=G)
                    sc = Chain(dve, share_chain, 1, s)
                    inverse_sum = sc.put(v.reciprocal(step_of(0), sums))
                if a.runs(GROUPS):
                    wait(dve, v_back[a.w], a.uses(4) * 16)
                    wait(dve, hv_T, a.g - 1)
                    wait(dve, share_ready, a.g + 1)
                    v.tensor_tensor(hv[:, a.u, :].rearrange("p (q c) -> p q c", c=HD),
                                    v_in[:, a.w, :].rearrange("p (q c) -> p q c", c=HD),
                                    share[:, a.u, 1, :].unsqueeze(2).to_broadcast([P, G * H, HD]), ALU.mult)\
                        .then_inc(hv_done, 1)
                if i.runs(GROUPS):
                    inverse = invert(i, c_fin_chain, c_std, c_applied)
                if b.runs(GROUPS):
                    wait(dve, o_mm, b.g + 1)
                    wait(dve, xd_back[b.w], b.uses(4) * 16)
                    wait(dve, c_applied, b.g - 1)
                    v.tensor_tensor(y[:, b.u, :], xd[:, b.w, :], bank[b.u][:, :], ALU.add).then_inc(c_y, 1)
                if i.runs(GROUPS):
                    shift(i, inverse, c_stats)
                if s.runs(GROUPS):
                    sc.see(inverse_sum)
                    v.tensor_tensor(step_of(1), sums, step_of(0), ALU.mult)\
                        .then_inc(share_ready, 1)
                if d.runs(GROUPS):
                    wait(dve, c_applied, d.g + 1)
                    wait(dve, sd_chain, d.g)
                    dot(res, v_dst, d, sd_chain)
                if b.runs(GROUPS):
                    c = Chain(dve, c_chain, 1, b)
                    wait(dve, c_y, b.g + 1)
                    stats = c.put(moments(b, y[:, b.u, :], range(G)))
                if d.runs(GROUPS):
                    keep_dots(s_dst, d, sd_chain, sd_done)
                if b.runs(GROUPS):
                    c.see(stats)
                    combine(b, range(G)).then_inc(c_var, 1)
            dve.wait_ge(sums_done, 1)
            all_done(dve, v_stored, 1)
            pipeline(dve, stage4, 5)
            all_done(dve, c_scat, G)
            fetch_indices(Step(-2), False, d_idx)
            fetch_indices(Step(-1), False, d_idx)

            def stage5(s):
                wait(dve, d_got[s.w], s.uses(4) * 16 * G)
                fetch_indices(s, False, d_idx)
                wait(dve, d_chain, s.g)
                dot(xs, v_src, s, d_chain)
                keep_dots(s_src, s, d_chain, d_done)
            pipeline(dve, stage5)

            v.memset(agg[:, 1, (G - 1) * D:G * D], 0.0)
            c = Chain(dve, att_chain, None)
            dve.wait_ge(d_done, GROUPS)
            c.link(v.tensor_tensor(logit[:, :], s_src[:, :], s_dst[:, :], ALU.add))
            c.link(v.scalar_tensor_tensor(logit2[:, :], logit[:, :], SLOPE, logit[:, :], ALU.mult, ALU.max))
            c.link(v.tensor_tensor(logit[:, :], logit2[:, :], pen_pad[:, :], ALU.add))
            v.tensor_reduce(max_p[:, :], logit[:, :], AX, ALU.max).then_inc(max_col, 1)
            dve.wait_ge(max_T, 1)
            v.tensor_reduce(max_all[:, :], bank[2][0:1, 0:P], AX, ALU.max).then_inc(max_one, 1)
            dve.wait_ge(max_b, 1)
            v.tensor_scalar(neg_max[:, :], bank[3][:, 0:1], -1.0, None, ALU.mult).then_inc(neg_ready, 1)
            dve.wait_ge(sum_b, 1)
            v.tensor_copy(chunkrow[:, :], bank[5][:, 0:P])
            c.link(v.reciprocal(inv_sum[:, :], bank[4][:, 0:1]))
            v.tensor_scalar(att[:, :], att[:, :], inv_sum[:, :], None, ALU.mult).then_inc(att_ready, 1)

            def stage7(s):
                a, b, i = s.back(1), s.back(2), s.back(3)
                rec, own = Chain(dve, r_chain, G, s), Chain(dve, own_chain, G, a)

                def running(t):
                    if not s.runs(GROUPS):
                        return
                    if t:
                        rec.see(t)
                        prev = T(agg, s.u, t - 1)
                    else:
                        wait(dve, xa_done, s.g + 1)
                        wait(dve, e_y, s.g - 1)
                        wait(dve, r_chain, s.g * G)
                        prev = T(agg, 1 - s.u, G - 1)
                    rec.put(v.scalar_tensor_tensor(T(agg, s.u, t), prev, same_prev[:, bass.ds(s.g * G + t, 1)],
                                                   T(xa, s.u, t), ALU.mult, ALU.add))

                def kept(t):
                    if a.runs(GROUPS):
                        wait(dve, own_chain, a.g * G + t)
                        own.put(v.scalar_tensor_tensor(part[:, :], T(agg, a.u, t),
                                                       first_last[:, bass.ds(a.g * G + t, 1)], part[:, :],
                                                       ALU.mult, ALU.add))
                running(0)
                if b.runs(GROUPS):
                    wait(dve, e_y, b.g + 1)
                    moments(b, bank[b.w], (0, 1))
                if i.runs(GROUPS):
                    inverse = invert(i, e_fin_chain, e_std, e_applied)
                running(1)
                if i.runs(GROUPS):
                    shift(i, inverse, e_stats)
                if b.runs(GROUPS):
                    c = Chain(dve, e_chain, 1, b)
                    c.put(moments(b, bank[b.w], (2, 3)))
                running(2)
                kept(0)
                running(3)
                kept(1)
                if b.runs(GROUPS):
                    c.see(1)
                    combine(b, (0, 1))
                kept(2)
                if b.runs(GROUPS):
                    combine(b, (2, 3)).then_inc(e_var, 1)
                kept(3)
            pipeline(dve, stage7, 3)

            c = Chain(dve, last_chain, None)
            dve.wait_ge(own_chain, GROUPS * G)
            dve.wait_ge(f_pe, 1)
            v.tensor_tensor_scan(carryT[:, 1:P + 1], chunkrow[:, :], bank[4][:, 0:P], 0.0, ALU.mult, ALU.add)\
                .then_inc(f_dve, 1)
            dve.wait_ge(f_pe, 2)
            v.tensor_tensor(total[:, :], part[:, :], bank[5][:, 0:P], ALU.add).then_inc(f_dve, 1)
            dve.wait_ge(f_dve, 2)
            dve.wait_ge(f_got, 16)
            dve.wait_ge(e_applied, GROUPS)
            c.link(v.tensor_tensor(y[:, 0, 0:D], x1c[:, :], total[:, :], ALU.add))
            c.link(v.bn_stats(yst[:, 0, :], y[:, 0, 0:D]))
            v.bn_aggr(ymv[:, 0, 0, :], yst[:, 0, :]).then_inc(f_dve, 1)
            dve.wait_ge(f_act, 1)
            c.link(v.reciprocal(ysc[:, 0, 0, 0:1], ystd[:, 0, 0:1]))
            v.scalar_tensor_tensor(ysc[:, 0, 1, 0:1], ymv[:, 0, 0, 0:1], -1.0, ysc[:, 0, 0, 0:1], ALU.mult, ALU.mult)\
                .then_inc(f_dve, 1)


_INS = ["x", "src", "dst", "edge_attr_64", "L0_gnn_Wq", "L0_gnn_bq", "L0_gnn_Wk", "L0_gnn_bk", "L0_gnn_Wv",
        "L0_gnn_bv", "L0_gnn_Wb", "L0_gnn_bb", "L0_gnn_Wo", "L0_gnn_bo", "L1_gnn_W", "L1_gnn_a"]


def kernel(**inputs):
    import numpy as np
    import concourse.bacc as bacc
    from concourse import mybir as mb
    from concourse.bass_utils import run_bass_kernel_spmd

    nc = bacc.Bacc("TRN2", target_bir_lowering=False, num_devices=1)
    arrays, args = {}, []
    for name in _INS:
        a = np.ascontiguousarray(inputs[name])
        arrays[f"in_{name}"] = a
        args.append(nc.dram_tensor(f"in_{name}", a.shape, mb.dt.from_np(a.dtype), kind="ExternalInput").ap())
    args.append(nc.dram_tensor("out_dram", inputs["x"].shape, mb.dt.float32, kind="ExternalOutput").ap())
    gnn_kernel(nc, *args)
    return run_bass_kernel_spmd(nc, [arrays], core_ids=[0]).results[0]["out_dram"]
```
